# Optimizing a Trainium2 kernel written in Bass

```python
import numpy as np
import jax
import jax.numpy as jnp

def _softmax(x, axis=-1):
    return jax.nn.softmax(x, axis=axis)

def _gelu(x):
    return jax.nn.gelu(x, approximate=True)

def _silu(x):
    return jax.nn.silu(x)

def _sigmoid(x):
    return jax.nn.sigmoid(x)

def _layernorm(x, axis=-1, eps=1e-05):
    m = jnp.mean(x, axis=axis, keepdims=True)
    v = jnp.var(x, axis=axis, keepdims=True)
    return (x - m) / jnp.sqrt(v + eps)

def _scatter_add(tgt, idx, src, axis=0):
    return tgt.at[idx].add(src)

def _segment_sum(src, seg, n):
    return jax.ops.segment_sum(src, seg, n)
kernel_name = 'mk_seq_postln_d1_jaxref_r8_c56b09'

def setup_inputs(seed: int=0):
    np.random.seed(seed)
    _w = jnp.asarray

    def _L0_attn_setup():
        import jax, jax.numpy as jnp
        import numpy as np
        B, T, DIM = (2, 128, 128)
        H, D = (16, 64)
        key = jax.random.key(seed)
        k1, k2, k3, k4 = jax.random.split(key, 4)
        s = DIM ** (-0.5)
        return {'x': jax.random.normal(k1, (B, T, DIM), jnp.float32), 'w_qkv': jax.random.normal(k2, (DIM, 3 * H * D), jnp.float32) * s, 'w_gate': jax.random.normal(k3, (DIM, H * D), jnp.float32) * s, 'w_out': jax.random.normal(k4, (H * D, DIM), jnp.float32) * s}
    _L0_attn_in = _L0_attn_setup()

    def _L0_ffn_setup():
        import jax, jax.numpy as jnp
        import numpy as np
        HIDDEN = 128
        NUM_EXPERTS = 8
        TOP_K = 2
        B, S = (2, 256)
        key = jax.random.key(seed)
        k1, k2, k3, k4, k5 = jax.random.split(key, 5)
        d, dff, E = (HIDDEN, 4 * HIDDEN, NUM_EXPERTS)
        x = jax.random.normal(k1, (B, S, d), dtype=jnp.float32)
        W1 = jax.random.normal(k2, (E, d, dff), dtype=jnp.float32) * (1.0 / np.sqrt(d))
        b1 = jax.random.normal(k3, (E, dff), dtype=jnp.float32) * 0.01
        W2 = jax.random.normal(k4, (E, dff, d), dtype=jnp.float32) * (1.0 / np.sqrt(dff))
        b2 = jax.random.normal(k5, (E, d), dtype=jnp.float32) * 0.01
        return {'x': x, 'W1': W1, 'b1': b1, 'W2': W2, 'b2': b2}
    _L0_ffn_in = _L0_ffn_setup()
    _d = {'L0_attn_x': _L0_attn_in['x'], 'L0_attn_w_qkv': _L0_attn_in['w_qkv'], 'L0_attn_w_gate': _L0_attn_in['w_gate'], 'L0_attn_w_out': _L0_attn_in['w_out'], 'L0_ffn_W1': _L0_ffn_in['W1'], 'L0_ffn_b1': _L0_ffn_in['b1'], 'L0_ffn_W2': _L0_ffn_in['W2'], 'L0_ffn_b2': _L0_ffn_in['b2']}
    _x0 = _d['L0_attn_x']
    _d['L0_attn_x'] = jax.random.normal(jax.random.fold_in(jax.random.key(seed), 1), (2, 1024, 128), dtype=_x0.dtype)
    del _x0
    return _d

def reference(L0_attn_x, L0_attn_w_qkv, L0_attn_w_gate, L0_attn_w_out, L0_ffn_W1, L0_ffn_b1, L0_ffn_W2, L0_ffn_b2):

    def _L0_attn_ref(x, w_qkv, w_gate, w_out):
        import jax, jax.numpy as jnp
        import numpy as np
        B, T, DIM = (2, 128, 128)
        H, D = (16, 64)
        b, t, c = x.shape
        qkv = (x @ w_qkv).reshape(b, t, 3, H, D)
        q, k, v = (qkv[:, :, 0], qkv[:, :, 1], qkv[:, :, 2])
        gate = jax.nn.sigmoid((x @ w_gate).reshape(b, t, H, D))
        q = jax.nn.elu(q) + 1.0
        k = jax.nn.elu(k) + 1.0
        k_cum = jnp.cumsum(k, axis=1)
        kv = jnp.cumsum(k[..., None, :] * v[..., :, None], axis=1)
        numerator = jnp.einsum('bthj,bthij->bthi', q, kv)
        denominator = jnp.einsum('bthj,bthj->bth', q, k_cum)
        out = numerator / (denominator[..., None] + 1e-06)
        out = out * gate
        return out.reshape(b, t, H * D) @ w_out

    def _L0_ffn_ref(x, W1, b1, W2, b2):
        import jax, jax.numpy as jnp
        import numpy as np
        HIDDEN = 128
        NUM_EXPERTS = 8
        TOP_K = 2
        B, S = (2, 256)
        Bm, Sm, d = x.shape
        E = W1.shape[0]
        x_flat = x.reshape(-1, d)
        h = jnp.mod(x_flat[:, :TOP_K].sum(axis=1).astype(jnp.int32), E)
        sel = jnp.stack([h, jnp.mod(h + 1, E)], axis=1)

        def step(acc, params):
            e, W1e, b1e, W2e, b2e = params
            w = jnp.any(sel == e, axis=1).astype(x.dtype) / TOP_K
            y = jnp.maximum(x_flat @ W1e + b1e, 0.0) @ W2e + b2e
            return (acc + w[:, None] * y, None)
        init = jnp.zeros_like(x_flat)
        out_flat, _ = jax.lax.scan(step, init, (jnp.arange(E), W1, b1, W2, b2))
        return out_flat.reshape(Bm, Sm, d)
    x = L0_attn_x
    x = _layernorm(x + _L0_attn_ref(x, L0_attn_w_qkv, L0_attn_w_gate, L0_attn_w_out), axis=-1)
    x = _layernorm(x + _L0_ffn_ref(x, L0_ffn_W1, L0_ffn_b1, L0_ffn_W2, L0_ffn_b2), axis=-1)
    return x

_drawn_inputs = setup_inputs


def setup_inputs(seed=0):
    import zlib

    import numpy as np

    out = dict(_drawn_inputs(seed))
    spreads = {}
    factors = {'L0_ffn_b1': 8.0, 'L0_ffn_b2': 8.0}
    for name, (base, spread) in spreads.items():
        noise = np.random.default_rng([zlib.crc32(name.encode()), seed]).standard_normal(out[name].shape)
        drawn = base * np.exp(spread * noise) if base else spread * noise
        out[name] = jnp.asarray(drawn.astype(out[name].dtype))
    for name, factor in factors.items():
        out[name] = (out[name] * factor).astype(out[name].dtype)
    return out
```

```python
from contextlib import ExitStack

import concourse.bass as bass
from concourse import mybir

F32 = mybir.dt.float32
F32R = mybir.dt.float32r
ALU = mybir.AluOpType
ACT = mybir.ActivationFunctionType

BF16 = mybir.dt.bfloat16
I32 = mybir.dt.int32
AX = mybir.AxisListType

P = 128
HEADS, HD = 16, 64
PAIRS = HEADS // 2
VW = HD + 1
LN_EPS = 1e-5
DEN_EPS = 1e-6


def build(nc, x, w_qkv, w_gate, w_out, ffn_w1, ffn_b1, ffn_w2, ffn_b2, out):
    B, T, D = x.shape
    NR = T // P
    NH = B * NR
    GROUPS = HEADS // 4
    HDALL = HEADS * HD
    E, _, F = ffn_w1.shape
    FB = F // P
    TILES = NH + E - 1
    NOWHERE = 2 * B * T
    WRAP = 3 * E
    assert 2 * (TILES // 2) + 1 == TILES and D == P and E & (E - 1) == 0
    x1_rows = nc.dram_tensor("x1_rows", (B * T, D), F32).ap()
    out_rows = out.rearrange("b t d -> (b t) d")

    with ExitStack() as ctx:
        def sb(name, shape, dt=F32):
            return ctx.enter_context(nc.sbuf_tensor(name, shape, dt))

        def pb(name):
            return ctx.enter_context(nc.psum_tensor(name, [P, 512], F32))

        def sem(name):
            return ctx.enter_context(nc.semaphore(name))

        ident = sb("ident", [P, P])
        causal = sb("causal", [P, P])
        w_full = sb("w_full", [P, 8, 512])
        w_hi = sb("w_hi", [P, 8, 512], F32R)
        w_lo = sb("w_lo", [P, 8, 512], F32R)
        wo = sb("wo", [P, PAIRS, P])
        x_in = [sb(f"x_in{b}", [P, P]) for b in range(B)]
        x_res = [sb(f"x_res{b}", [P, P]) for b in range(B)]
        xt_hi = [sb(f"xt_hi{b}", [P, P], F32R) for b in range(B)]
        xt_lo = [sb(f"xt_lo{b}", [P, P], F32R) for b in range(B)]
        expo = [sb(f"expo{i}", [P, 512]) for i in range(2)]
        relu = [sb(f"relu{i}", [P, 512]) for i in range(2)]
        qd = [sb(f"qd{b}", [P, PAIRS, 2, P]) for b in range(B)]
        kt = [sb(f"kt{b}", [P, PAIRS, P]) for b in range(B)]
        ktok = sb("ktok", [P, PAIRS, P])
        v1 = [sb(f"v1_{b}", [P, HEADS, VW]) for b in range(B)]
        gate = [sb(f"gate{b}", [P, HEADS, HD]) for b in range(B)]
        probs = [sb(f"probs{i}", [P, 4, P]) for i in range(2)]
        den = [sb(f"den{i}", [P, 4, 1]) for i in range(2)]
        rden = [sb(f"rden{i}", [P, 4, 1]) for i in range(2)]
        num = [sb(f"num{i}", [P, 4, HD]) for i in range(2)]
        og = sb("og", [P, HEADS, HD])
        ogt = sb("ogt", [P, PAIRS, P])
        state = [sb(f"state{b}", [P, PAIRS, 2, VW]) for b in range(B)]
        z = sb("z", [P, P])
        stats = sb("stats", [P, 6])
        mv = sb("mv", [P, 2])
        rstd = sb("rstd", [P, 1])
        veps = sb("veps", [P, 1])
        eps = sb("eps", [P, 1])
        minus_half = sb("minus_half", [P, 1])
        x1 = sb("x1", [P, NH, P])

        w1_stage = [sb(f"w1_stage{i}", [P, F]) for i in range(2)]
        w1_tab = sb("w1_tab", [P, E, 2, F], F32R)
        w2_tab = w_full[:].rearrange("p e (f d) -> p e f d", f=FB)
        b1_rows = sb("b1_rows", [E * FB, P])
        b1_tab = sb("b1_tab", [P, E, FB])
        b2_all = sb("b2_all", [P, E, D])
        b2_sum = sb("b2_sum", [P, E, D])
        b2_tab = sb("b2_tab", [P, E, D])
        half_col = sb("half_col", [P, 1])

        before = sb("before", [P, P], BF16)
        ones_bf = sb("ones_bf", [P, P], BF16)
        iota_e = sb("iota_e", [P, E])
        iota_p = sb("iota_p", [P, P])
        iota_k = sb("iota_k", [P, TILES])
        iota_c = sb("iota_c", [P, NH, 1])
        row_no = sb("row_no", [P, 1])
        lower_e = sb("lower_e", [P, E, E])
        rt = [sb(f"rt{i}", [P, NH]) for i in range(8)]
        rt_int = sb("rt_int", [P, NH], I32)
        rt_low = sb("rt_low", [P, NH], I32)
        onehot = sb("onehot", [P, NH, E], BF16)
        tot = sb("tot", [P, E])
        over = sb("over", [P, E, NH])
        tiles_of = sb("tiles_of", [P, E])
        low_prod = sb("low_prod", [P, E, E])
        first_tile = sb("first_tile", [P, E])
        place3 = sb("place3", [P, NH, E])
        place4 = sb("place4", [P, NH, E])
        at_row = sb("at_row", [P, NH, P], BF16)
        at_tile = sb("at_tile", [P, NH, 3, TILES], BF16)
        found = sb("found", [P, 3, TILES])
        idx_f = sb("idx_f", [P, TILES])
        gaps = sb("gaps", [P, TILES])
        idx_from = sb("idx_from", [P, TILES], I32)
        idx_to = sb("idx_to", [P, TILES], I32)
        reached = sb("reached", [P, TILES, E])
        exp_f = sb("exp_f", [P, TILES])
        reached_int = sb("reached_int", [P, TILES], I32)
        expert = sb("expert", [P, 2, TILES], I32)

        idx_g = [sb(f"idx_g{i}", [P, 1], I32) for i in range(2)]
        idx_s = [sb(f"idx_s{i}", [P, 1], I32) for i in range(2)]
        xg = [sb(f"xg{i}", [P, P]) for i in range(2)]
        xg_res = [sb(f"xg_res{i}", [P, P]) for i in range(2)]
        xg_hi = [sb(f"xg_hi{i}", [P, P], F32R) for i in range(2)]
        xg_lo = [sb(f"xg_lo{i}", [P, P], F32R) for i in range(2)]
        w1_now = [[w_hi[:, 4 * i + 2 * j:4 * i + 2 * j + 2, :] for j in range(2)] for i in range(2)]
        b1_now = [[sb(f"b1_now{i}{j}", [P, FB]) for j in range(2)] for i in range(2)]
        hid = [[expo[0], expo[1]], [relu[0], relu[1]]]
        z2 = sb("z2", [P, P])
        y2 = [sb(f"y2_{i}", [P, P]) for i in range(2)]

        ps_p = [pb(f"ps_p{i}") for i in range(2)]
        ps_s = [pb(f"ps_s{i}") for i in range(2)]
        ps_o = [pb(f"ps_o{i}") for i in range(2)]
        ps_t = pb("ps_t")
        ps_m = pb("ps_m")

        w_in = [sem(f"w_in{i}") for i in range(8)]
        wo_in = sem("wo_in")
        x_in_sem = [sem(f"x_in_sem{b}") for b in range(B)]
        x_res_sem = [sem(f"x_res_sem{b}") for b in range(B)]
        consts = sem("consts")
        route_fill, route_consts = sem("route_fill"), sem("route_consts")
        pool_consts = sem("pool_consts")
        veps_ready = sem("veps_ready")
        filled = sem("filled")
        w_hi_ready = sem("w_hi_ready")
        w_ready = sem("w_ready")
        pe_xt, xt_half, xt_ready = sem("pe_xt"), sem("xt_half"), sem("xt_ready")
        pe_qk, exp_done, qk_ready = sem("pe_qk"), sem("exp_done"), sem("qk_ready")
        pe_v, v_ready, pe_g, gate_ready = sem("pe_v"), sem("v_ready"), sem("pe_g"), sem("gate_ready")
        pe_s, probs_ready = sem("pe_s"), sem("probs_ready")
        pe_kt, ktok_ready = sem("pe_kt"), sem("ktok_ready")
        pe_o, den_ready, rden_ready, num_ready, og_ready = (
            sem("pe_o"), sem("den_ready"), sem("rden_ready"), sem("num_ready"), sem("og_ready"))
        pe_kv, state_ready = sem("pe_kv"), sem("state_ready")
        pe_ot, ogt_ready = sem("pe_ot"), sem("ogt_ready")
        pe_y, z_ready, stats_ready, mv_ready, rstd_ready, x1_ready = (
            sem("pe_y"), sem("z_ready"), sem("stats_ready"), sem("mv_ready"), sem("rstd_ready"), sem("x1_ready"))
        x1_out = [sem(f"x1_out{b}") for b in range(B)]
        w2_in, b1_in, b2_in, w1_in = sem("w2_in"), sem("b1_in"), sem("b2_in"), [sem(f"w1_in{i}") for i in range(2)]
        w1_hi_done, w1_split, b2_added, b2_ready = sem("w1_hi_done"), sem("w1_split"), sem("b2_added"), sem("b2_ready")
        b1_turned, b1_ready = sem("b1_turned"), sem("b1_ready")
        route, onehot_ready, ranked, places_ready, listed, experts_ready, indices_ready = (
            sem("route"), sem("onehot_ready"), sem("ranked"), sem("places_ready"), sem("listed"),
            sem("experts_ready"), sem("indices_ready"))
        idx_g_ready, idx_s_ready = sem("idx_g_ready"), sem("idx_s_ready")
        xg_in = [sem(f"xg_in{i}") for i in range(2)]
        xg_turned, xg_half, xg_ready, xg_kept = sem("xg_turned"), sem("xg_half"), sem("xg_ready"), sem("xg_kept")
        w1_now_ready = [sem(f"w1_now_ready{j}") for j in range(2)]
        pe_h, pe_f = sem("pe_h"), sem("pe_f")
        hid_ready = [sem(f"hid_ready{j}") for j in range(2)]
        z2_ready, stats2_ready, mv2_ready, veps2_ready, rstd2_ready, y2_ready = (
            sem("z2_ready"), sem("stats2_ready"), sem("mv2_ready"), sem("veps2_ready"), sem("rstd2_ready"), sem("y2_ready"))
        y2_out = [sem(f"y2_out{i}") for i in range(2)]

        block = ctx.enter_context(nc.Block())

        KV_LOTS = [(0, 3), (3, 3), (6, 2)]

        def after(eng, s, value):
            if not (isinstance(value, int) and value <= 0):
                eng.wait_ge(s, value)

        def tile_loop(eng, body):
            for k in range(3):
                body(k, k % 2, k // 2)
            with eng.Fori(1, TILES // 2 - 1) as i:
                body(2 * i + 1, 1, i)
                body(2 * i + 2, 0, i + 1)
            body(TILES - 2, 1, TILES // 2 - 1)
            body(TILES - 1, 0, TILES // 2)

        def wait_alone(eng, s, value, held, count):
            if not isinstance(value, int):
                value = eng.snap(eng.to_reg(value))
            eng.wait_ge(held, count)
            eng.wait_ge(s, value)

        def more(k):
            return not isinstance(k, int) or k + 1 < TILES

        @block.sync
        def _(sp):
            def load_x(r, b):
                sp.dma_start(x_in[b][:], x[b, bass.ts(r, P), :]).then_inc(x_in_sem[b], 16)

            def load_res(r, b):
                sp.dma_start(x_res[b][:], x[b, bass.ts(r, P), :]).then_inc(x_res_sem[b], 16)

            load_x(0, 0)
            for g in range(GROUPS):
                for part in range(2):
                    sp.dma_start(w_full[:, g, 256 * part:256 * part + 256],
                                 w_qkv[:, HDALL * part + 256 * g:HDALL * part + 256 * g + 256]).then_inc(w_in[g], 16)
            load_x(0, 1)
            for j in range(2):
                sp.dma_start(w_full[:, 4 + j, :], w_qkv[:, 2 * HDALL + 512 * j:2 * HDALL + 512 * j + 512]).then_inc(w_in[4 + j], 16)
            for j in range(2):
                sp.dma_start(w_full[:, 6 + j, :], w_gate[:, 512 * j:512 * j + 512]).then_inc(w_in[6 + j], 16)
            sp.dma_start(wo[:], w_out.rearrange("(j p) d -> p j d", p=P)).then_inc(wo_in, 16)
            for b in range(B):
                load_res(0, b)
            sp.dma_start(b1_rows[:], ffn_b1.rearrange("e (f p) -> (e f) p", p=P)).then_inc(b1_in, 16)
            sp.dma_start(b2_all[:].rearrange("p e d -> p (e d)"),
                         ffn_b2.rearrange("(o e) d -> o (e d)", o=1).broadcast_to([P, E * D])).then_inc(b2_in, 16)
            sp.wait_ge(w_ready, 8)
            sp.dma_start(w2_tab, ffn_w2.rearrange("e (f p) d -> p e f d", p=P)).then_inc(w2_in, 16)

            def store(r, b):
                sp.wait_ge(x1_ready, 2 * r + b + 1)
                sp.dma_start(x1_rows[bass.ts(r + NR * b, P), :], x1[:, 2 * r + b, :]).then_inc(x1_out[b], 16)

            with sp.Fori(0, NR - 1) as r:
                for b in range(B):
                    sp.wait_ge(pe_xt, 2 * r + b + 1)
                    load_x(r + 1, b)
                    store(r, b)
                    load_res(r + 1, b)
            for b in range(B):
                store(NR - 1, b)
            for i in range(2):
                sp.wait_ge(y2_out[i], 16 * (TILES // 2 + 1 - i))

        @block.gpsimd
        def _(pool):
            nc.gpsimd.memset(ident[:], 0.0).then_inc(filled, 1)
            nc.gpsimd.memset(causal[:], 1.0).then_inc(filled, 1)
            pool.wait_ge(filled, 2)
            nc.gpsimd.affine_select(out=ident[:], in_=ident[:], compare_op=ALU.not_equal, fill=1.0, base=0,
                                    pattern=[[-1, P]], channel_multiplier=1).then_inc(consts, 1)
            nc.gpsimd.affine_select(out=causal[:], in_=causal[:], compare_op=ALU.is_ge, fill=0.0, base=0,
                                    pattern=[[1, P]], channel_multiplier=-1).then_inc(consts, 1)
            nc.gpsimd.memset(half_col[:], 0.5).then_inc(pool_consts, 1)
            nc.gpsimd.memset(eps[:], LN_EPS).then_inc(pool_consts, 1)
            nc.gpsimd.memset(minus_half[:], -0.5).then_inc(pool_consts, 1)
            for b in range(B):
                nc.gpsimd.memset(qd[b][:], 0.0).then_inc(consts, 1)
                nc.gpsimd.memset(v1[b][:, :, HD:VW], 1.0).then_inc(consts, 1)

            nc.gpsimd.memset(ones_bf[:], 1.0).then_inc(route_fill, 1)
            pool.wait_ge(route_fill, 1)
            nc.gpsimd.affine_select(out=before[:], in_=ones_bf[:], compare_op=ALU.is_gt, fill=0.0, base=0,
                                    pattern=[[1, P]], channel_multiplier=-1).then_inc(route_consts, 1)
            for dst, step, count, per_row in ((iota_e, 1, E, 0), (iota_p, 1, P, 0), (iota_k, P, TILES, 0), (row_no, 1, 1, 1)):
                nc.gpsimd.iota(dst[:], pattern=[[step, count]], base=0, channel_multiplier=per_row,
                               allow_small_or_imprecise_dtypes=True).then_inc(route_consts, 1)
            for b in range(B):
                nc.gpsimd.iota(iota_c[:, b::2, :], pattern=[[1, NR], [0, 1]], base=NR * b, channel_multiplier=0,
                               allow_small_or_imprecise_dtypes=True).then_inc(route_consts, 1)

            def load_w1(e):
                after(pool, w1_split, e - 1)
                pool.dma_start(w1_stage[e % 2][:], ffn_w1[e]).then_inc(w1_in[e % 2], 16)

            def split_w1(e):
                pool.wait_ge(w1_in[e % 2], 16 * (e // 2 + 1))
                nc.gpsimd.tensor_copy(w1_tab[:, e, 0, :], w1_stage[e % 2][:]).then_inc(w1_hi_done, 1)
                pool.wait_ge(w1_hi_done, e + 1)
                nc.gpsimd.tensor_tensor(w1_tab[:, e, 1, :], w1_stage[e % 2][:], w1_tab[:, e, 0, :].bitcast(F32),
                                        ALU.subtract).then_inc(w1_split, 1)
                if e + 2 < E:
                    load_w1(e + 2)

            def mean_b2():
                pool.wait_ge(b2_in, 16)
                nc.gpsimd.tensor_tensor(b2_sum[:, 1:E, :], b2_all[:, 0:E - 1, :], b2_all[:, 1:E, :], ALU.add).then_inc(b2_added, 1)
                nc.gpsimd.tensor_tensor(b2_sum[:, 0, :], b2_all[:, E - 1, :], b2_all[:, 0, :], ALU.add).then_inc(b2_added, 1)
                pool.wait_ge(b2_added, 2)
                nc.gpsimd.tensor_tensor(b2_tab[:], b2_sum[:], half_col[:].unsqueeze(2).broadcast_to([P, E, D]),
                                        ALU.mult).then_inc(b2_ready, 1)

            def divide(n, g):
                pool.wait_ge(num_ready, 4 * n + g + 1)
                after(pool, pe_ot, 2 * n - 1 + g // 2)
                nc.gpsimd.tensor_tensor(og[:, 4 * g:4 * g + 4, :], num[g % 2][:],
                                        rden[g % 2][:].broadcast_to([P, 4, HD]), ALU.mult).then_inc(og_ready, 1)

            def deviation(n):
                pool.wait_ge(mv_ready, n + 1)
                nc.gpsimd.tensor_tensor(veps[:], mv[:, 1:2], eps[:], ALU.add).then_inc(veps_ready, 1)
                pool.wait_ge(veps_ready, n + 1)
                nc.gpsimd.tensor_tensor(rstd[:], veps[:], minus_half[:], ALU.pow).then_inc(rstd_ready, 1)

            def half(r, b):
                for g in range(GROUPS):
                    divide(2 * r + b, g)
                deviation(2 * r + b)

            pool.wait_ge(pool_consts, 3)
            for e in range(2):
                load_w1(e)
            for b in range(B):
                half(0, b)
                for e in range(b * E // 2, (b + 1) * E // 2):
                    split_w1(e)
            mean_b2()
            with pool.Fori(1, NR) as r:
                for b in range(B):
                    half(r, b)

            def gather(k, i, turn):
                after(pool, xg_turned, k - 1)
                after(pool, xg_kept, k - 1)
                nc.gpsimd.tensor_copy(idx_g[i][:], idx_from[:, bass.ds(k, 1)]).then_inc(idx_g_ready, 1)
                wait_alone(pool, idx_g_ready, k + 1, pool_consts, 3)
                nc.gpsimd.indirect_dma_start(xg[i][:], None, x1_rows, bass.IndirectOffsetOnAxis(ap=idx_g[i][:], axis=0),
                                             bounds_check=B * T - 1, oob_is_err=True).then_inc(xg_in[i], 16)

            def deviation2(k):
                pool.wait_ge(mv2_ready, k + 1)
                nc.gpsimd.tensor_tensor(veps[:], mv[:, 1:2], eps[:], ALU.add).then_inc(veps2_ready, 1)
                pool.wait_ge(veps2_ready, k + 1)
                nc.gpsimd.tensor_tensor(rstd[:], veps[:], minus_half[:], ALU.pow).then_inc(rstd2_ready, 1)

            def scatter(k, i, turn):
                after(pool, y2_out[i], 16 * turn)
                nc.gpsimd.tensor_copy(idx_s[i][:], idx_to[:, bass.ds(k, 1)]).then_inc(idx_s_ready, 1)
                wait_alone(pool, y2_ready, k + 1, pool_consts, 3)
                pool.wait_ge(idx_s_ready, k + 1)
                nc.gpsimd.indirect_dma_start(out_rows, bass.IndirectOffsetOnAxis(ap=idx_s[i][:], axis=0), y2[i][:], None,
                                             bounds_check=B * T - 1, oob_is_err=False).then_inc(y2_out[i], 16)

            pool.wait_ge(indices_ready, 2)
            for b in range(B):
                pool.wait_ge(x1_out[b], 16 * NR)
            gather(0, 0, 0)
            gather(1, 1, 0)

            def body(k, i, turn):
                if not isinstance(k, int) or k + 2 < TILES:
                    gather(k + 2, i, turn + 1)
                if not isinstance(k, int) or k >= 1:
                    deviation2(k - 1)
                    scatter(k - 1, 1 - i, turn - 1 + i)

            tile_loop(pool, body)
            deviation2(TILES - 1)
            scatter(TILES - 1, (TILES - 1) % 2, (TILES - 1) // 2)

        @block.scalar
        def _(act):
            for i in range(8):
                act.wait_ge(w_in[i], 32 if i < 4 else 16)
                nc.scalar.activation(w_hi[:, i, :], w_full[:, i, :], ACT.Copy).then_inc(w_hi_ready, 1)

            def exps(m, g):
                act.wait_ge(pe_qk, 4 * m + g + 1)
                after(act, qk_ready, 4 * m + g - 1)
                nc.scalar.activation(expo[g % 2][:], ps_p[g % 2][:], ACT.Exp)
                nc.scalar.activation(relu[g % 2][:], ps_p[g % 2][:], ACT.Relu).then_inc(exp_done, 1)

            def values(m, b, j):
                act.wait_ge(pe_v, 2 * m + j + 1)
                nc.scalar.activation(v1[b][:, 8 * j:8 * j + 8, 0:HD],
                                     ps_p[j % 2][:].rearrange("p (h d) -> p h d", d=HD), ACT.Copy).then_inc(v_ready, 1)

            def gates(m, b, j):
                act.wait_ge(pe_g, 2 * m + j + 1)
                nc.scalar.activation(gate[b][:, 8 * j:8 * j + 8, :],
                                     ps_p[j % 2][:].rearrange("p (h d) -> p h d", d=HD), ACT.Tanh, scale=0.5).then_inc(gate_ready, 1)

            def keys(n, j):
                act.wait_ge(pe_kt, 2 * n + j + 1)
                nc.scalar.activation(ktok[:, 4 * j:4 * j + 4, :], ps_t[:].rearrange("p (a s) -> p a s", s=P),
                                     ACT.Copy).then_inc(ktok_ready, 1)

            def outs(n, j):
                act.wait_ge(pe_ot, 2 * n + j + 1)
                after(act, pe_y, n)
                nc.scalar.activation(ogt[:, 4 * j:4 * j + 4, :], ps_t[:].rearrange("p (a s) -> p a s", s=P),
                                     ACT.Copy).then_inc(ogt_ready, 1)

            def half(r, b, project):
                n = 2 * r + b
                for g in range(GROUPS):
                    if project:
                        exps(n + 1, g)
                    if g < 2:
                        keys(n, g)
                if project:
                    values(n + 1, 1 - b, 0)
                    values(n + 1, 1 - b, 1)
                outs(n, 0)
                if project:
                    gates(n + 1, 1 - b, 0)
                outs(n, 1)
                if project:
                    gates(n + 1, 1 - b, 1)

            for g in range(GROUPS):
                exps(0, g)
            for j in range(2):
                values(0, 0, j)
            for j in range(2):
                gates(0, 0, j)
            for b in range(B):
                half(0, b, True)
            with act.Fori(1, NR - 1) as r:
                for b in range(B):
                    half(r, b, True)
            for b in range(B):
                half(NR - 1, b, b < B - 1)

            def fetch(k, i):
                after(act, pe_h, 2 * k - 3)
                after(act, hid_ready[0], k - 1)
                e = act.value_load(expert[0:1, 0, bass.ds(k, 1)], min_val=0, max_val=E - 1)
                nc.scalar.activation(b1_now[i][0][:], b1_tab[:, bass.ds(e, 1), :].rearrange("p o f -> p (o f)"), ACT.Copy)
                nc.scalar.activation(w1_now[i][0], w1_tab[:, bass.ds(e, 1), :, :].rearrange("p o h f -> p (o h) f").bitcast(F32),
                                     ACT.Copy).then_inc(w1_now_ready[0], 1)

            def hidden(k, i):
                act.wait_ge(w1_now_ready[0], k + 1)
                after(act, pe_f, 2 * k - 3)
                act.wait_ge(pe_h, 2 * k + 1)
                for f in range(FB):
                    cols = slice(f * P, f * P + P)
                    last = nc.scalar.activation(hid[i][0][:, cols], ps_p[0][:, cols], ACT.Relu, bias=b1_now[i][0][:, f:f + 1])
                last.then_inc(hid_ready[0], 1)

            def body(k, i, turn):
                if more(k):
                    fetch(k + 1, 1 - i)
                hidden(k, i)

            act.wait_ge(experts_ready, 1)
            act.wait_ge(b1_ready, 1)
            act.wait_ge(w1_split, E)
            fetch(0, 0)
            tile_loop(act, body)

        @block.vector
        def _(dve):
            def split_x(m, b):
                dve.wait_ge(pe_xt, m + 1)
                nc.vector.tensor_copy(xt_hi[b][:], ps_m[:, P:2 * P]).then_inc(xt_half, 1)
                dve.wait_ge(xt_half, m + 1)
                nc.vector.tensor_tensor(xt_lo[b][:], ps_m[:, P:2 * P], xt_hi[b][:].bitcast(F32), ALU.subtract).then_inc(xt_ready, 1)

            def rows(m, b, g):
                dve.wait_ge(exp_done, 4 * m + g + 1)
                cut = lambda t, a: t.rearrange("p (a s) -> p a s", s=P)[:, a:a + 2, :]
                up, e = relu[g % 2], expo[g % 2]
                nc.vector.scalar_tensor_tensor(kt[b][:, 2 * g:2 * g + 2, :], cut(e[:], 2), 1.0, cut(up[:], 2), ALU.min, ALU.add)
                for i, rows_of in enumerate((slice(0, HD), slice(HD, P))):
                    last = nc.vector.scalar_tensor_tensor(qd[b][rows_of, 2 * g:2 * g + 2, i, :], cut(e[rows_of, :], 0), 1.0,
                                                          cut(up[rows_of, :], 0), ALU.min, ALU.add)
                last.then_inc(qk_ready, 1)

            def mask(n, g):
                dve.wait_ge(pe_s, 4 * n + g + 1)
                after(dve, pe_o, 4 * n + g - 1)
                nc.vector.tensor_tensor(probs[g % 2][:], ps_s[g % 2][:].rearrange("p (h t) -> p h t", t=P),
                                        causal[:].unsqueeze(1).broadcast_to([P, 4, P]), ALU.mult).then_inc(probs_ready, 1)

            def numerator(n, b, g):
                i = 4 * n + g
                heads = ps_o[g % 2][:, 0:4 * VW].rearrange("p (h d) -> p h d", d=VW)
                dve.wait_ge(pe_o, i + 1)
                after(dve, og_ready, i - 1)
                nc.vector.tensor_scalar(den[g % 2][:], heads[:, :, HD:VW], 2.0, 2 * DEN_EPS, ALU.mult, ALU.add).then_inc(den_ready, 1)
                dve.wait_ge(den_ready, i + 1)
                nc.vector.reciprocal(rden[g % 2][:], den[g % 2][:]).then_inc(rden_ready, 1)
                dve.wait_ge(gate_ready, 2 * n + g // 2 + 1)
                nc.vector.scalar_tensor_tensor(num[g % 2][:], gate[b][:, 4 * g:4 * g + 4, :], 1.0,
                                               heads[:, :, 0:HD], ALU.add, ALU.mult).then_inc(num_ready, 1)

            def add_state(n, b, i, first):
                a, k = KV_LOTS[i]
                lot = state[b][:, a:a + k, :, :].rearrange("p a h d -> p (a h d)")
                dve.wait_ge(pe_kv, 3 * n + i + 1)
                if first:
                    nc.vector.tensor_copy(lot, ps_t[:, 0:2 * VW * k]).then_inc(state_ready, 1)
                else:
                    dve.wait_ge(state_ready, 3 * n + i - 5)
                    nc.vector.tensor_tensor(lot, ps_t[:, 0:2 * VW * k], lot, ALU.add).then_inc(state_ready, 1)

            def norm(r, b):
                n = 2 * r + b
                dve.wait_ge(pe_y, n + 1)
                dve.wait_ge(x_res_sem[b], 16 * r + 16)
                nc.vector.tensor_tensor(z[:], ps_m[:, 0:P], x_res[b][:], ALU.add).then_inc(z_ready, 1)
                dve.wait_ge(z_ready, n + 1)
                nc.vector.bn_stats(stats[:], z[:]).then_inc(stats_ready, 1)
                dve.wait_ge(consts, 1)
                dve.wait_ge(stats_ready, n + 1)
                nc.vector.bn_aggr(mv[:], stats[:]).then_inc(mv_ready, 1)
                dve.wait_ge(rstd_ready, n + 1)
                nc.vector.tensor_scalar(x1[:, n, :], z[:], mv[:, 0:1], rstd[:, 0:1], ALU.subtract, ALU.mult).then_inc(x1_ready, 1)

            def half(r, b, first, project, split):
                n = 2 * r + b
                for g in range(GROUPS):
                    mask(n, g)
                    if project:
                        rows(n + 1, 1 - b, g)
                    if g >= 1:
                        numerator(n, b, g - 1)
                    if g >= 2:
                        add_state(n, b, g - 2, first)
                numerator(n, b, 3)
                add_state(n, b, 2, first)
                if split:
                    split_x(n + 2, b)
                norm(r, b)

            dve.wait_ge(consts, 1)
            split_x(0, 0)
            for i in range(8):
                dve.wait_ge(w_hi_ready, i + 1)
                nc.vector.tensor_tensor(w_lo[:, i, :], w_full[:, i, :], w_hi[:, i, :].bitcast(F32), ALU.subtract).then_inc(w_ready, 1)
                if i == 0:
                    split_x(1, 1)
                    dve.wait_ge(consts, 6)
                if 1 <= i <= 4:
                    rows(0, 0, i - 1)
            for b in range(B):
                half(0, b, True, True, True)
            with dve.Fori(1, NR - 1) as r:
                for b in range(B):
                    half(r, b, False, True, True)
            for b in range(B):
                half(NR - 1, b, False, b < B - 1, False)

            steps = [0]

            def then(ins):
                steps[0] += 1
                ins.then_inc(route, 1)
                dve.wait_ge(route, steps[0])

            v = nc.vector
            dve.wait_ge(x1_ready, NH)
            dve.wait_ge(route_consts, 5 + B)
            s, a, whole, up, sign, h, place, row = (t[:] for t in rt)
            then(v.tensor_tensor(s, x1[:, :, 0], x1[:, :, 1], ALU.add))
            then(v.scalar_tensor_tensor(a, s, -1.0, s, ALU.mult, ALU.max))
            then(v.tensor_copy(rt_int[:], a))
            then(v.tensor_copy(whole, rt_int[:]))
            then(v.tensor_tensor(up, whole, a, ALU.is_gt))
            then(v.tensor_tensor(whole, whole, up, ALU.subtract))
            then(v.tensor_scalar(sign, s, 0.0, -2.0, ALU.is_lt, ALU.mult))
            then(v.scalar_tensor_tensor(h, sign, 1.0, whole, ALU.add, ALU.mult))
            then(v.tensor_scalar(rt_int[:], h, float(WRAP), None, ALU.add))
            then(v.tensor_scalar(rt_low[:], rt_int[:], E - 1, None, ALU.bitwise_and))
            then(v.tensor_copy(h, rt_low[:]))
            v.tensor_tensor(onehot[:], h.unsqueeze(2).broadcast_to([P, NH, E]),
                            iota_e[:].unsqueeze(1).broadcast_to([P, NH, E]), ALU.is_equal).then_inc(onehot_ready, 1)
            then(v.tensor_tensor(lower_e[:], iota_e[:].unsqueeze(2).broadcast_to([P, E, E]),
                                 iota_e[:].unsqueeze(1).broadcast_to([P, E, E]), ALU.is_gt))
            dve.wait_ge(ranked, 1)
            then(v.tensor_tensor(over[:], ps_s[1][:, 0:E].unsqueeze(2).broadcast_to([P, E, NH]),
                                 iota_k[:, 0:NH].unsqueeze(1).broadcast_to([P, E, NH]), ALU.is_gt))
            then(v.tensor_reduce(tiles_of[:], over[:], AX.X, ALU.add))
            then(v.tensor_tensor(low_prod[:], lower_e[:], tiles_of[:].unsqueeze(1).broadcast_to([P, E, E]), ALU.mult))
            then(v.tensor_reduce(tot[:], low_prod[:], AX.X, ALU.add))
            then(v.tensor_scalar(first_tile[:], tot[:], float(P), None, ALU.mult))
            then(v.tensor_tensor(place3[:], ps_s[0][:, 0:NH * E].rearrange("p (n e) -> p n e", e=E),
                                 first_tile[:].unsqueeze(1).broadcast_to([P, NH, E]), ALU.add))
            then(v.tensor_tensor(place4[:], place3[:], onehot[:], ALU.mult))
            then(v.tensor_reduce(place, place4[:], AX.X, ALU.add))
            then(v.tensor_copy(rt_int[:], place))
            then(v.tensor_scalar(rt_low[:], rt_int[:], P - 1, None, ALU.bitwise_and))
            then(v.tensor_copy(row, rt_low[:]))
            then(v.tensor_tensor(place, place, row, ALU.subtract))
            then(v.tensor_tensor(at_tile[:, :, 0, :], place.unsqueeze(2).broadcast_to([P, NH, TILES]),
                                 iota_k[:].unsqueeze(1).broadcast_to([P, NH, TILES]), ALU.is_equal))
            v.tensor_scalar(at_tile[:, :, 1, :], at_tile[:, :, 0, :], row_no[:, 0:1], None, ALU.mult)
            v.tensor_tensor(at_tile[:, :, 2, :], at_tile[:, :, 0, :], iota_c[:].broadcast_to([P, NH, TILES]), ALU.mult)
            for n in range(NH):
                last = v.tensor_scalar(at_row[:, n, :], iota_p[:], row[:, n:n + 1], None, ALU.is_equal)
            last.then_inc(places_ready, 1)
            then(v.tensor_tensor(reached[:], iota_k[:].unsqueeze(2).broadcast_to([P, TILES, E]),
                                 first_tile[:].unsqueeze(1).broadcast_to([P, TILES, E]), ALU.is_ge))
            then(v.tensor_reduce(exp_f[:], reached[:], AX.X, ALU.add))
            then(v.tensor_copy(reached_int[:], exp_f[:]))
            then(v.tensor_scalar(expert[:, 0, :], exp_f[:], -1.0, None, ALU.add))
            v.tensor_scalar(expert[:, 1, :], reached_int[:], E - 1, None, ALU.bitwise_and).then_inc(experts_ready, 1)
            dve.wait_ge(listed, 1)
            then(v.tensor_copy(found[:].rearrange("p a k -> p (a k)"), ps_m[:, 0:3 * TILES]))
            then(v.scalar_tensor_tensor(idx_f[:], found[:, 2, :], float(P), found[:, 1, :], ALU.mult, ALU.add))
            v.tensor_copy(idx_from[:], idx_f[:]).then_inc(indices_ready, 1)
            then(v.tensor_scalar(gaps[:], found[:, 0, :], -float(NOWHERE), float(NOWHERE), ALU.mult, ALU.add))
            then(v.tensor_tensor(gaps[:], gaps[:], idx_f[:], ALU.add))
            v.tensor_copy(idx_to[:], gaps[:]).then_inc(indices_ready, 1)
            dve.wait_ge(b1_turned, 1)
            v.tensor_copy(b1_tab[:].rearrange("p e f -> p (e f)"), ps_o[0][:, 0:E * FB]).then_inc(b1_ready, 1)
            dve.wait_ge(b1_ready, 1)
            dve.wait_ge(b2_ready, 1)
            dve.wait_ge(w1_split, E)
            dve.wait_ge(experts_ready, 1)

            def take(k, i):
                after(dve, pe_h, 2 * k - 2)
                after(dve, hid_ready[1], k - 1)
                e = dve.value_load(expert[0:1, 1, bass.ds(k, 1)], min_val=0, max_val=E - 1)
                v.tensor_copy(b1_now[i][1][:], b1_tab[:, bass.ds(e, 1), :].rearrange("p o f -> p (o f)"))
                v.tensor_copy(w1_now[i][1], w1_tab[:, bass.ds(e, 1), :, :].rearrange("p o h f -> p (o h) f").bitcast(F32))\
                    .then_inc(w1_now_ready[1], 1)
                dve.wait_ge(xg_turned, k + 1)
                v.tensor_copy(xg_hi[i][:], ps_t[:, 0:P]).then_inc(xg_half, 1)
                dve.wait_ge(xg_half, k + 1)
                v.tensor_tensor(xg_lo[i][:], ps_t[:, 0:P], xg_hi[i][:].bitcast(F32), ALU.subtract).then_inc(xg_ready, 1)
                return e

            def keep(k, i, e):
                dve.wait_ge(xg_in[i], 16 * ((k - i) // 2 + 1) if isinstance(k, int) else 8 * (k - i) + 16)
                after(dve, z2_ready, k - 1)
                v.tensor_tensor(xg_res[i][:], xg[i][:], b2_tab[:, bass.ds(e, 1), :].rearrange("p o d -> p (o d)"),
                                ALU.add).then_inc(xg_kept, 1)

            def hidden(k, i):
                dve.wait_ge(w1_now_ready[1], k + 1)
                after(dve, pe_f, 2 * k - 2)
                dve.wait_ge(pe_h, 2 * k + 2)
                for f in range(FB):
                    cols = slice(f * P, f * P + P)
                    last = v.tensor_scalar(hid[i][1][:, cols], ps_p[1][:, cols], b1_now[i][1][:, f:f + 1], 0.0, ALU.add, ALU.max)
                last.then_inc(hid_ready[1], 1)

            def moments(k, i):
                dve.wait_ge(pe_f, 2 * k + 2)
                dve.wait_ge(xg_kept, k + 1)
                after(dve, y2_ready, k)
                v.scalar_tensor_tensor(z2[:], ps_o[i][:, 0:P], 0.5, xg_res[i][:], ALU.mult, ALU.add).then_inc(z2_ready, 1)
                dve.wait_ge(z2_ready, k + 1)
                v.bn_stats(stats[:], z2[:]).then_inc(stats2_ready, 1)
                dve.wait_ge(experts_ready, 1)
                dve.wait_ge(stats2_ready, k + 1)
                v.bn_aggr(mv[:], stats[:]).then_inc(mv2_ready, 1)

            def finish(k, i, turn):
                dve.wait_ge(rstd2_ready, k + 1)
                after(dve, y2_out[i], 16 * turn)
                v.tensor_scalar(y2[i][:], z2[:], mv[:, 0:1], rstd[:, 0:1], ALU.subtract, ALU.mult).then_inc(y2_ready, 1)

            def body(k, i, turn):
                if more(k):
                    e = take(k + 1, 1 - i)
                if not isinstance(k, int) or k >= 2:
                    finish(k - 2, i, turn - 1)
                hidden(k, i)
                if not isinstance(k, int) or k >= 1:
                    moments(k - 1, 1 - i)
                if more(k):
                    keep(k + 1, 1 - i, e)

            keep(0, 0, take(0, 0))
            tile_loop(dve, body)
            finish(TILES - 2, 1, TILES // 2 - 1)
            moments(TILES - 1, 0)
            finish(TILES - 1, 0, TILES // 2)

        @block.tensor
        def _(pe):
            def turn_x(m, b, loads, before=None):
                pe.wait_ge(x_in_sem[b], loads)
                if before is not None:
                    after(pe, *before)
                nc.tensor.transpose(ps_m[:, P:2 * P], x_in[b][:], ident[:]).then_inc(pe_xt, 1)

            def three(dst, pairs):
                for i, (lhs, rhs) in enumerate(pairs):
                    last = nc.tensor.matmul(dst, lhs, rhs, start=(i == 0), stop=(i == 2))
                return last

            def project_qk(m, b, g):
                if g == 0:
                    pe.wait_ge(xt_ready, m + 1)
                    after(pe, gate_ready, 2 * m - 1)
                elif g == 1:
                    after(pe, gate_ready, 2 * m)
                else:
                    pe.wait_ge(exp_done, 4 * m + g - 1)
                for i in range(4):
                    hi, lo = w_hi[:, g, i * P:i * P + P], w_lo[:, g, i * P:i * P + P]
                    last = three(ps_p[g % 2][:, i * P:i * P + P],
                                 [(hi, xt_hi[b][:]), (hi, xt_lo[b][:]), (lo, xt_hi[b][:])])
                last.then_inc(pe_qk, 1)

            def project_vg(m, b, i):
                j = i % 2
                if i < 2:
                    pe.wait_ge(exp_done, 4 * m + 3 + j)
                else:
                    pe.wait_ge(v_ready, 2 * m + 1 + j)
                hi, lo = w_hi[:, 4 + i, :], w_lo[:, 4 + i, :]
                three(ps_p[j][:], [(xt_hi[b][:], hi), (xt_hi[b][:], lo), (xt_lo[b][:], hi)]).then_inc(pe_v if i < 2 else pe_g, 1)

            def scores(n, b, g):
                pe.wait_ge(qk_ready, 4 * n + g + 1)
                after(pe, probs_ready, 4 * n + g - 1)
                for j in range(2):
                    a = 2 * g + j
                    last = nc.tensor.matmul(ps_s[g % 2][:, 256 * j:256 * j + 256], kt[b][:, a, :],
                                            qd[b][:, a, :, :].rearrange("p h t -> p (h t)"), start=True, stop=True)
                last.then_inc(pe_s, 1)

            def turn_k(n, b, j):
                after(pe, *((ogt_ready, 2 * n) if j == 0 else (ktok_ready, 2 * n + 1)))
                for i in range(4):
                    last = nc.tensor.transpose(ps_t[:, i * P:i * P + P], kt[b][:, 4 * j + i, :], ident[:])
                last.then_inc(pe_kt, 1)

            def attend(n, b, g, first):
                after(pe, num_ready, 4 * n + g - 1)
                pe.wait_ge(v_ready, 2 * n + g // 2 + 1)
                if not first:
                    pe.wait_ge(state_ready, 3 * n - 3)
                pe.wait_ge(probs_ready, 4 * n + g + 1)
                for i in range(4):
                    h = 4 * g + i
                    dst = ps_o[g % 2][:, i * VW:i * VW + VW]
                    if not first:
                        nc.tensor.matmul(dst, qd[b][:, h // 2, h % 2, :], state[b][:, h // 2, h % 2, :], start=True, stop=False)
                    last = nc.tensor.matmul(dst, probs[g % 2][:, i, :], v1[b][:, h, :], start=first, stop=True)
                last.then_inc(pe_o, 1)

            def sum_kv(n, b, i):
                a, k = KV_LOTS[i]
                if i == 0:
                    pe.wait_ge(ktok_ready, 2 * n + 2)
                    pe.wait_ge(v_ready, 2 * n + 2)
                else:
                    pe.wait_ge(state_ready, 3 * n + i)
                for j in range(k):
                    last = nc.tensor.matmul(ps_t[:, 2 * VW * j:2 * VW * (j + 1)], ktok[:, a + j, :],
                                            v1[b][:, 2 * (a + j):2 * (a + j) + 2, :].rearrange("p h d -> p (h d)"),
                                            start=True, stop=True)
                last.then_inc(pe_kv, 1)

            def turn_o(n, j):
                pe.wait_ge(og_ready, 4 * n + 2 * j + 2)
                pe.wait_ge(*((state_ready, 3 * n + 3) if j == 0 else (ogt_ready, 2 * n + 1)))
                for i in range(4):
                    a = 4 * j + i
                    last = nc.tensor.transpose(ps_t[:, i * P:i * P + P],
                                               og[:, 2 * a:2 * a + 2, :].rearrange("p h d -> p (h d)"), ident[:])
                last.then_inc(pe_ot, 1)

            def project_out(n, m_split):
                pe.wait_ge(ogt_ready, 2 * n + 2)
                after(pe, *((xt_ready, n + 3) if m_split else (z_ready, n)))
                for a in range(PAIRS):
                    last = nc.tensor.matmul(ps_m[:, 0:P], ogt[:, a, :], wo[:, a, :], start=(a == 0), stop=(a == PAIRS - 1))
                last.then_inc(pe_y, 1)

            def half(r, b, first, project, split):
                n = 2 * r + b
                for g in range(GROUPS):
                    scores(n, b, g)
                    if project:
                        project_qk(n + 1, 1 - b, g)
                    if g >= 1:
                        attend(n, b, g - 1, first)
                    if g < 2:
                        turn_k(n, b, g)
                    else:
                        sum_kv(n, b, g - 2)
                if project:
                    project_vg(n + 1, 1 - b, 0)
                attend(n, b, 3, first)
                if project:
                    project_vg(n + 1, 1 - b, 1)
                sum_kv(n, b, 2)
                turn_o(n, 0)
                if project:
                    project_vg(n + 1, 1 - b, 2)
                if split:
                    turn_x(n + 2, b, 16 * r + 32, (z_ready, n))
                turn_o(n, 1)
                if project:
                    project_vg(n + 1, 1 - b, 3)
                project_out(n, split)

            pe.wait_ge(consts, 1)
            turn_x(0, 0, 16)
            turn_x(1, 1, 16, (xt_ready, 1))
            for g in range(GROUPS):
                pe.wait_ge(w_ready, g + 1)
                project_qk(0, 0, g)
            for i in range(4):
                pe.wait_ge(w_ready, 5 + i)
                project_vg(0, 0, i)
            pe.wait_ge(wo_in, 16)
            for b in range(B):
                half(0, b, True, True, True)
            with pe.Fori(1, NR - 1) as r:
                for b in range(B):
                    half(r, b, False, True, True)
            for b in range(B):
                half(NR - 1, b, False, b < B - 1, False)

            pe.wait_ge(b1_in, 16)
            nc.tensor.transpose(ps_o[0][:, 0:E * FB], b1_rows[:], ident[0:E * FB, 0:E * FB]).then_inc(b1_turned, 1)
            pe.wait_ge(onehot_ready, 1)
            rows = onehot[:].rearrange("p n e -> p (n e)")
            nc.tensor.matmul(ps_s[0][:, 0:NH * E], before[:], rows, start=True, stop=False, skip_group_check=True)
            for d in range(1, NH):
                nc.tensor.matmul(ps_s[0][:, d * E:NH * E], ones_bf[:], rows[:, 0:(NH - d) * E], start=False, stop=(d == NH - 1),
                                 skip_group_check=True)
            for n in range(NH):
                last = nc.tensor.matmul(ps_s[1][:, 0:E], ones_bf[:], onehot[:, n, :], start=(n == 0), stop=(n == NH - 1))
            last.then_inc(ranked, 1)
            pe.wait_ge(places_ready, 1)
            for n in range(NH):
                last = nc.tensor.matmul(ps_m[:, 0:3 * TILES], at_row[:, n, :], at_tile[:, n, :, :].rearrange("p a k -> p (a k)"),
                                        start=(n == 0), stop=(n == NH - 1))
            last.then_inc(listed, 1)

            def turn_rows(k, i, turn):
                pe.wait_ge(xg_in[i], 16 * turn + 16)
                after(pe, xg_ready, k)
                nc.tensor.transpose(ps_t[:, 0:P], xg[i][:], ident[:]).then_inc(xg_turned, 1)

            def into_hidden(k, i, j):
                pe.wait_ge(xg_ready, k + 1)
                pe.wait_ge(w1_now_ready[j], k + 1)
                after(pe, hid_ready[j], k)
                for f in range(FB):
                    hi, lo = (w1_now[i][j][:, part, f * P:f * P + P] for part in range(2))
                    last = three(ps_p[j][:, f * P:f * P + P], [(hi, xg_hi[i][:]), (hi, xg_lo[i][:]), (lo, xg_hi[i][:])])
                last.then_inc(pe_h, 1)

            def out_of_hidden(k, i, j, e):
                if j == 0:
                    after(pe, z2_ready, k - 1)
                pe.wait_ge(hid_ready[j], k + 1)
                for f in range(FB):
                    last = nc.tensor.matmul(ps_o[i][:, 0:P], hid[i][j][:, f * P:f * P + P],
                                            w2_tab[:, bass.ds(e, 1), f, :].rearrange("p o d -> p (o d)"),
                                            start=(j == 0 and f == 0), stop=(j == 1 and f == FB - 1))
                last.then_inc(pe_f, 1)

            def experts_of(k):
                return [pe.value_load(expert[0:1, j, bass.ds(k, 1)], min_val=0, max_val=E - 1) for j in range(2)]

            def body(k, i, turn):
                first = isinstance(k, int) and k == 0
                pair = None if first else experts_of(k - 1)
                if more(k):
                    turn_rows(k + 1, 1 - i, turn + i)
                for j in range(2):
                    into_hidden(k, i, j)
                    if not first:
                        out_of_hidden(k - 1, 1 - i, j, pair[j])

            pe.wait_ge(experts_ready, 1)
            pe.wait_ge(w2_in, 16)
            pe.wait_ge(b1_ready, 1)
            turn_rows(0, 0, 0)
            tile_loop(pe, body)
            pair = experts_of(TILES - 1)
            for j in range(2):
                out_of_hidden(TILES - 1, 0, j, pair[j])


_INS = ["L0_attn_x", "L0_attn_w_qkv", "L0_attn_w_gate", "L0_attn_w_out",
        "L0_ffn_W1", "L0_ffn_b1", "L0_ffn_W2", "L0_ffn_b2"]
_OUTS = [((2, 1024, 128), "float32")]


def kernel(**inputs):
    import numpy as _np
    import concourse.bacc as _bacc
    from concourse import mybir as _mybir
    from concourse.bass_utils import run_bass_kernel_spmd as _run

    nc = _bacc.Bacc("TRN2", target_bir_lowering=False, num_devices=1)
    arrays, args = {}, []
    for name in _INS:
        a = _np.ascontiguousarray(inputs[name])
        arrays[f"in_{name}_dram"] = a
        args.append(nc.dram_tensor(f"in_{name}_dram", a.shape, _mybir.dt.from_np(a.dtype), kind="ExternalInput").ap())
    for i, (shape, dtype) in enumerate(_OUTS):
        dt = _mybir.dt.from_np(_np.dtype(dtype))
        args.append(nc.dram_tensor(f"out_{i}_dram", shape, dt, kind="ExternalOutput").ap())
    build(nc, *args)
    r = _run(nc, [arrays], core_ids=[0])
    got = tuple(r.results[0][f"out_{i}_dram"] for i in range(len(_OUTS)))
    return got[0]
```

```python
from contextlib import ExitStack

import concourse.bass as bass
from concourse import mybir

F32 = mybir.dt.float32
F32R = mybir.dt.float32r
ALU = mybir.AluOpType
ACT = mybir.ActivationFunctionType

BF16 = mybir.dt.bfloat16
I32 = mybir.dt.int32
AX = mybir.AxisListType

P = 128
HEADS, HD = 16, 64
PAIRS = HEADS // 2
VW = HD + 1
LN_EPS = 1e-5
DEN_EPS = 1e-6


def build(nc, x, w_qkv, w_gate, w_out, ffn_w1, ffn_b1, ffn_w2, ffn_b2, out):
    B, T, D = x.shape
    NR = T // P
    NH = B * NR
    GROUPS = HEADS // 4
    HDALL = HEADS * HD
    E, _, F = ffn_w1.shape
    FB = F // P
    TILES = NH + E - 1
    NOWHERE = 2 * B * T
    WRAP = 3 * E
    assert TILES % 4 == 3 and D == P and E & (E - 1) == 0
    x1_rows = nc.dram_tensor("x1_rows", (B * T, D), F32).ap()
    out_rows = out.rearrange("b t d -> (b t) d")

    with ExitStack() as ctx:
        def sb(name, shape, dt=F32):
            return ctx.enter_context(nc.sbuf_tensor(name, shape, dt))

        def pb(name):
            return ctx.enter_context(nc.psum_tensor(name, [P, 512], F32))

        def sem(name):
            return ctx.enter_context(nc.semaphore(name))

        ident = sb("ident", [P, P])
        causal = sb("causal", [P, P])
        w_full = sb("w_full", [P, 8, 512])
        w_hi = sb("w_hi", [P, 8, 512], F32R)
        w_lo = sb("w_lo", [P, 8, 512], F32R)
        wo = sb("wo", [P, PAIRS, P])
        x_in = sb("x_in", [P, B, P])
        x_res = [sb(f"x_res{b}", [P, P]) for b in range(B)]
        xt_hi = sb("xt_hi", [P, B, P], F32R)
        xt_lo = sb("xt_lo", [P, B, P], F32R)
        expo = [sb(f"expo{i}", [P, 512]) for i in range(2)]
        relu = [sb(f"relu{i}", [P, 512]) for i in range(2)]
        qk = sb("qk", [P, PAIRS, 2, B, P])
        ktok = sb("ktok", [P, PAIRS, P])
        v1 = [sb(f"v1_{b}", [P, HEADS, VW]) for b in range(B)]
        gate = [sb(f"gate{b}", [P, HEADS, HD]) for b in range(B)]
        probs = [sb(f"probs{i}", [P, 4, P]) for i in range(2)]
        den = [sb(f"den{i}", [P, 4, 1]) for i in range(2)]
        rden = [sb(f"rden{i}", [P, 4, 1]) for i in range(2)]
        num = [sb(f"num{i}", [P, 4, HD]) for i in range(2)]
        og = sb("og", [P, HEADS, HD])
        ogt = sb("ogt", [P, PAIRS, P])
        state = [sb(f"state{b}", [P, PAIRS, 2, VW]) for b in range(B)]
        z = sb("z", [P, P])
        stats = sb("stats", [P, 6])
        mv = sb("mv", [P, 2])
        rstd = sb("rstd", [P, 1])
        veps = sb("veps", [P, 1])
        eps = sb("eps", [P, 1])
        minus_half = sb("minus_half", [P, 1])
        x1 = sb("x1", [P, NH, P])

        w1_tab = sb("w1_tab", [P, E, F])
        w2_tab = sb("w2_tab", [P, E, FB, D])
        b1_rows = sb("b1_rows", [E * FB, P])
        b1_tab = sb("b1_tab", [P, E, FB])
        b2_all = sb("b2_all", [P, E, D])
        b2_sum = sb("b2_sum", [P, E, D])
        b2_tab = sb("b2_tab", [P, E, D])
        half_col = sb("half_col", [P, 1])

        before = sb("before", [P, P], BF16)
        ones_bf = sb("ones_bf", [P, P], BF16)
        iota_e = sb("iota_e", [P, E])
        iota_p = sb("iota_p", [P, P])
        iota_k = sb("iota_k", [P, TILES])
        iota_c = sb("iota_c", [P, NH, 1])
        row_no = sb("row_no", [P, 1])
        lower_e = sb("lower_e", [P, E, E])
        rt = [sb(f"rt{i}", [P, NH]) for i in range(8)]
        rt_int = sb("rt_int", [P, NH], I32)
        rt_low = sb("rt_low", [P, NH], I32)
        onehot = sb("onehot", [P, NH, E], BF16)
        tot = sb("tot", [P, E])
        over = sb("over", [P, E, NH])
        tiles_of = sb("tiles_of", [P, E])
        low_prod = sb("low_prod", [P, E, E])
        first_tile = sb("first_tile", [P, E])
        place3 = sb("place3", [P, NH, E])
        place4 = sb("place4", [P, NH, E])
        at_row = sb("at_row", [P, NH, P], BF16)
        at_tile = sb("at_tile", [P, NH, 3, TILES], BF16)
        found = sb("found", [P, 3, TILES])
        idx_f = sb("idx_f", [P, TILES])
        gaps = sb("gaps", [P, TILES])
        idx_from = sb("idx_from", [P, TILES], I32)
        idx_to = sb("idx_to", [P, TILES], I32)
        reached = sb("reached", [P, TILES, E])
        exp_f = sb("exp_f", [P, TILES])
        reached_int = sb("reached_int", [P, TILES], I32)
        expert = sb("expert", [P, 2, TILES], I32)

        idx_g = [sb(f"idx_g{i}", [P, 1], I32) for i in range(4)]
        idx_s = [sb(f"idx_s{i}", [P, 1], I32) for i in range(2)]
        xg = [sb(f"xg{i}", [P, P]) for i in range(4)]
        xg_res = [sb(f"xg_res{i}", [P, P]) for i in range(2)]
        xgt = [sb(f"xgt{i}", [P, P]) for i in range(2)]
        w1_now = [[sb(f"w1_now{i}{j}", [P, F]) for j in range(2)] for i in range(2)]
        b1_now = [[sb(f"b1_now{i}{j}", [P, FB]) for j in range(2)] for i in range(2)]
        hid = [[expo[0], expo[1]], [relu[0], relu[1]]]
        z2 = sb("z2", [P, P])
        y2 = [sb(f"y2_{i}", [P, P]) for i in range(2)]

        ps_p = [pb(f"ps_p{i}") for i in range(2)]
        ps_s = [pb(f"ps_s{i}") for i in range(2)]
        ps_o = [pb(f"ps_o{i}") for i in range(2)]
        ps_t = pb("ps_t")
        ps_m = pb("ps_m")

        w_in = [sem(f"w_in{i}") for i in range(8)]
        wo_in = sem("wo_in")
        x_in_sem = sem("x_in_sem")
        x_res_sem = [sem(f"x_res_sem{b}") for b in range(B)]
        consts = sem("consts")
        ones_set = sem("ones_set")
        route_fill, route_consts = sem("route_fill"), sem("route_consts")
        pool_consts = sem("pool_consts")
        veps_ready = sem("veps_ready")
        filled = sem("filled")
        w_hi_ready = sem("w_hi_ready")
        w_ready = sem("w_ready")
        pe_xt, xt_half, xt_ready = sem("pe_xt"), sem("xt_half"), sem("xt_ready")
        pe_qk, exp_done, qk_ready = sem("pe_qk"), sem("exp_done"), sem("qk_ready")
        pe_v, v_ready, pe_g, gate_ready = sem("pe_v"), sem("v_ready"), sem("pe_g"), sem("gate_ready")
        pe_s, probs_ready = sem("pe_s"), sem("probs_ready")
        pe_kt, ktok_ready = sem("pe_kt"), sem("ktok_ready")
        pe_o, den_ready, rden_ready, num_ready, og_ready = (
            sem("pe_o"), sem("den_ready"), sem("rden_ready"), sem("num_ready"), sem("og_ready"))
        pe_kv, state_ready = sem("pe_kv"), sem("state_ready")
        pe_ot, ogt_ready = sem("pe_ot"), sem("ogt_ready")
        pe_y, z_ready, stats_ready, mv_ready, rstd_ready, x1_ready = (
            sem("pe_y"), sem("z_ready"), sem("stats_ready"), sem("mv_ready"), sem("rstd_ready"), sem("x1_ready"))
        x1_out = [sem(f"x1_out{b}") for b in range(B)]
        w1_in, w2_in, b1_in, b2_in = sem("w1_in"), sem("w2_in"), sem("b1_in"), sem("b2_in")
        zeroed, b2_added, b2_ready = sem("zeroed"), sem("b2_added"), sem("b2_ready")
        b1_turned, b1_ready = sem("b1_turned"), sem("b1_ready")
        route, onehot_ready, ranked, places_ready, listed, experts_ready, indices_ready = (
            sem("route"), sem("onehot_ready"), sem("ranked"), sem("places_ready"), sem("listed"),
            sem("experts_ready"), sem("indices_ready"))
        idx_g_ready, idx_s_ready = sem("idx_g_ready"), sem("idx_s_ready")
        xg_in = [sem(f"xg_in{i}") for i in range(4)]
        xg_turned, xgt_ready, xg_kept = sem("xg_turned"), sem("xgt_ready"), sem("xg_kept")
        w1_now_ready = [sem(f"w1_now_ready{j}") for j in range(2)]
        pe_h, pe_f = sem("pe_h"), sem("pe_f")
        hid_ready = [sem(f"hid_ready{j}") for j in range(2)]
        z2_ready, stats2_ready, mv2_ready, veps2_ready, rstd2_ready, y2_ready = (
            sem("z2_ready"), sem("stats2_ready"), sem("mv2_ready"), sem("veps2_ready"), sem("rstd2_ready"), sem("y2_ready"))
        y2_out = [sem(f"y2_out{i}") for i in range(2)]

        block = ctx.enter_context(nc.Block())

        KV_LOTS = [(0, 3), (3, 3), (6, 2)]

        def after(eng, s, value):
            if not (isinstance(value, int) and value <= 0):
                eng.wait_ge(s, value)

        class Tile:

            def __init__(self, i, c):
                self.i, self.c, self.k = i, c, 4 * i + c
                self.slot4, self.slot2 = c % 4, c % 2
                self.turn4, self.turn2 = i + c // 4, 2 * i + c // 2

            def plus(self, d):
                return Tile(self.i, self.c + d)

            def exists(self):
                return not isinstance(self.k, int) or 0 <= self.k < TILES

        def tile_loop(eng, body):
            for c in range(3):
                body(Tile(0, c))
            with eng.Fori(0, TILES // 4 - 1) as i:
                for c in range(3, 7):
                    body(Tile(i, c))
            for c in range(TILES - 4, TILES):
                body(Tile(0, c))

        def wait_alone(eng, s, value, held, count):
            if not isinstance(value, int):
                value = eng.snap(eng.to_reg(value))
            eng.wait_ge(held, count)
            eng.wait_ge(s, value)

        @block.sync
        def _(sp):
            def load_x(r):
                sp.dma_start(x_in[:], x[:, bass.ts(r, P), :].rearrange("b p d -> p b d")).then_inc(x_in_sem, 16)

            def load_res(r, b):
                sp.dma_start(x_res[b][:], x[b, bass.ts(r, P), :]).then_inc(x_res_sem[b], 16)

            def store(r, b):
                sp.wait_ge(x1_ready, 2 * r + b + 1)
                sp.dma_start(x1_rows[bass.ts(r + NR * b, P), :], x1[:, 2 * r + b, :]).then_inc(x1_out[b], 16)

            load_x(0)
            for g in range(GROUPS):
                for part in range(2):
                    sp.dma_start(w_full[:, g, 256 * part:256 * part + 256],
                                 w_qkv[:, HDALL * part + 256 * g:HDALL * part + 256 * g + 256]).then_inc(w_in[g], 16)
            for j in range(2):
                sp.dma_start(w_full[:, 4 + j, :], w_qkv[:, 2 * HDALL + 512 * j:2 * HDALL + 512 * j + 512]).then_inc(w_in[4 + j], 16)
            for j in range(2):
                sp.dma_start(w_full[:, 6 + j, :], w_gate[:, 512 * j:512 * j + 512]).then_inc(w_in[6 + j], 16)
            sp.wait_ge(pe_xt, 1)
            load_x(1)
            for b in range(B):
                load_res(0, b)
            sp.dma_start(wo[:], w_out.rearrange("(j p) d -> p j d", p=P)).then_inc(wo_in, 16)
            sp.dma_start(b1_rows[:], ffn_b1.rearrange("e (f p) -> (e f) p", p=P)).then_inc(b1_in, 16)
            sp.dma_start(b2_all[:].rearrange("p e d -> p (e d)"),
                         ffn_b2.rearrange("(o e) d -> o (e d)", o=1).broadcast_to([P, E * D])).then_inc(b2_in, 16)
            sp.dma_start(w1_tab[:], ffn_w1.rearrange("e p f -> p e f")).then_inc(w1_in, 16)
            sp.dma_start(w2_tab[:], ffn_w2.rearrange("e (f p) d -> p e f d", p=P)).then_inc(w2_in, 16)

            def rounds(r, ahead):
                if ahead:
                    sp.wait_ge(pe_xt, r + 2)
                    load_x(r + 2)
                for b in range(B):
                    store(r, b)
                    load_res(r + 1, b)

            with sp.Fori(0, NR - 2) as r:
                rounds(r, True)
            rounds(NR - 2, False)
            for b in range(B):
                store(NR - 1, b)
            for i in range(2):
                sp.wait_ge(y2_out[i], 16 * (TILES // 2 + 1 - i))

        @block.gpsimd
        def _(pool):
            nc.gpsimd.memset(ident[:], 0.0).then_inc(filled, 1)
            nc.gpsimd.memset(causal[:], 1.0).then_inc(filled, 1)
            pool.wait_ge(filled, 2)
            nc.gpsimd.affine_select(out=ident[:], in_=ident[:], compare_op=ALU.not_equal, fill=1.0, base=0,
                                    pattern=[[-1, P]], channel_multiplier=1).then_inc(consts, 1)
            nc.gpsimd.affine_select(out=causal[:], in_=causal[:], compare_op=ALU.is_ge, fill=0.0, base=0,
                                    pattern=[[1, P]], channel_multiplier=-1).then_inc(consts, 1)
            nc.gpsimd.memset(half_col[:], 0.5).then_inc(pool_consts, 1)
            nc.gpsimd.memset(eps[:], LN_EPS).then_inc(pool_consts, 1)
            nc.gpsimd.memset(minus_half[:], -0.5).then_inc(pool_consts, 1)
            for b in range(B):
                nc.gpsimd.memset(v1[b][:, :, HD:VW], 1.0).then_inc(ones_set, 1)
            for b in range(B):
                nc.gpsimd.memset(state[b][:], 0.0).then_inc(zeroed, 1)
            nc.gpsimd.memset(ones_bf[:], 1.0).then_inc(route_fill, 1)
            pool.wait_ge(route_fill, 1)
            nc.gpsimd.affine_select(out=before[:], in_=ones_bf[:], compare_op=ALU.is_gt, fill=0.0, base=0,
                                    pattern=[[1, P]], channel_multiplier=-1).then_inc(route_consts, 1)
            for dst, step, count, per_row in ((iota_e, 1, E, 0), (iota_p, 1, P, 0), (iota_k, P, TILES, 0), (row_no, 1, 1, 1)):
                nc.gpsimd.iota(dst[:], pattern=[[step, count]], base=0, channel_multiplier=per_row,
                               allow_small_or_imprecise_dtypes=True).then_inc(route_consts, 1)
            for b in range(B):
                nc.gpsimd.iota(iota_c[:, b::2, :], pattern=[[1, NR], [0, 1]], base=NR * b, channel_multiplier=0,
                               allow_small_or_imprecise_dtypes=True).then_inc(route_consts, 1)

            def mean_b2():
                pool.wait_ge(b2_in, 16)
                nc.gpsimd.tensor_tensor(b2_sum[:, 1:E, :], b2_all[:, 0:E - 1, :], b2_all[:, 1:E, :], ALU.add).then_inc(b2_added, 1)
                nc.gpsimd.tensor_tensor(b2_sum[:, 0, :], b2_all[:, E - 1, :], b2_all[:, 0, :], ALU.add).then_inc(b2_added, 1)
                pool.wait_ge(b2_added, 2)
                nc.gpsimd.tensor_tensor(b2_tab[:], b2_sum[:], half_col[:].unsqueeze(2).broadcast_to([P, E, D]),
                                        ALU.mult).then_inc(b2_ready, 1)

            def divide(n, g):
                pool.wait_ge(num_ready, 4 * n + g + 1)
                after(pool, pe_ot, 2 * n - 1 + g // 2)
                nc.gpsimd.tensor_tensor(og[:, 4 * g:4 * g + 4, :], num[g % 2][:],
                                        rden[g % 2][:].broadcast_to([P, 4, HD]), ALU.mult).then_inc(og_ready, 1)

            def deviation(n):
                pool.wait_ge(mv_ready, n + 1)
                nc.gpsimd.tensor_tensor(veps[:], mv[:, 1:2], eps[:], ALU.add).then_inc(veps_ready, 1)
                pool.wait_ge(veps_ready, n + 1)
                nc.gpsimd.tensor_tensor(rstd[:], veps[:], minus_half[:], ALU.pow).then_inc(rstd_ready, 1)

            def half(r, b):
                n = 2 * r + b
                if b or not isinstance(r, int) or r:
                    deviation(n - 1)
                for g in range(GROUPS):
                    divide(n, g)

            pool.wait_ge(pool_consts, 3)
            mean_b2()
            for b in range(B):
                half(0, b)
            with pool.Fori(1, NR) as r:
                for b in range(B):
                    half(r, b)

            deviation(NH - 1)

            def gather(t):
                k = t.k
                after(pool, xg_turned, k - 3)
                after(pool, xg_kept, k - 3)
                nc.gpsimd.tensor_copy(idx_g[t.slot4][:], idx_from[:, bass.ds(k, 1)]).then_inc(idx_g_ready, 1)
                wait_alone(pool, idx_g_ready, k + 1, pool_consts, 3)
                nc.gpsimd.indirect_dma_start(xg[t.slot4][:], None, x1_rows,
                                             bass.IndirectOffsetOnAxis(ap=idx_g[t.slot4][:], axis=0),
                                             bounds_check=B * T - 1, oob_is_err=True).then_inc(xg_in[t.slot4], 16)

            def deviation2(k):
                pool.wait_ge(mv2_ready, k + 1)
                nc.gpsimd.tensor_tensor(veps[:], mv[:, 1:2], eps[:], ALU.add).then_inc(veps2_ready, 1)
                pool.wait_ge(veps2_ready, k + 1)
                nc.gpsimd.tensor_tensor(rstd[:], veps[:], minus_half[:], ALU.pow).then_inc(rstd2_ready, 1)

            def scatter(t):
                k, i = t.k, t.slot2
                after(pool, y2_out[i], 16 * t.turn2)
                nc.gpsimd.tensor_copy(idx_s[i][:], idx_to[:, bass.ds(k, 1)]).then_inc(idx_s_ready, 1)
                wait_alone(pool, y2_ready, k + 1, pool_consts, 3)
                pool.wait_ge(idx_s_ready, k + 1)
                nc.gpsimd.indirect_dma_start(out_rows, bass.IndirectOffsetOnAxis(ap=idx_s[i][:], axis=0), y2[i][:], None,
                                             bounds_check=B * T - 1, oob_is_err=False).then_inc(y2_out[i], 16)

            pool.wait_ge(indices_ready, 2)
            for b in range(B):
                pool.wait_ge(x1_out[b], 16 * NR)
            for c in range(3):
                gather(Tile(0, c))

            def body(t):
                if t.plus(3).exists():
                    gather(t.plus(3))
                if t.plus(-1).exists():
                    deviation2(t.k - 1)
                    scatter(t.plus(-1))

            tile_loop(pool, body)
            deviation2(TILES - 1)
            scatter(Tile(0, TILES - 1))

        @block.scalar
        def _(act):
            def weights(i):
                act.wait_ge(w_in[i], 32 if i < 4 else 16)
                nc.scalar.activation(w_hi[:, i, :], w_full[:, i, :], ACT.Copy).then_inc(w_hi_ready, 1)

            def exps(r, f):
                act.wait_ge(pe_qk, 8 * r + f + 1)
                after(act, qk_ready, 8 * r + f - 1)
                nc.scalar.activation(expo[f % 2][:], ps_p[f % 2][:], ACT.Exp)
                nc.scalar.activation(relu[f % 2][:], ps_p[f % 2][:], ACT.Relu).then_inc(exp_done, 1)

            def values(m, b, j):
                act.wait_ge(pe_v, 2 * m + j + 1)
                nc.scalar.activation(v1[b][:, 8 * j:8 * j + 8, 0:HD],
                                     ps_p[j % 2][:].rearrange("p (h d) -> p h d", d=HD), ACT.Copy).then_inc(v_ready, 1)

            def gates(m, b, j):
                act.wait_ge(pe_g, 2 * m + j + 1)
                nc.scalar.activation(gate[b][:, 8 * j:8 * j + 8, :],
                                     ps_p[j % 2][:].rearrange("p (h d) -> p h d", d=HD), ACT.Tanh, scale=0.5).then_inc(gate_ready, 1)

            def keys(n, j):
                act.wait_ge(pe_kt, 2 * n + j + 1)
                nc.scalar.activation(ktok[:, 4 * j:4 * j + 4, :], ps_t[:].rearrange("p (a s) -> p a s", s=P),
                                     ACT.Copy).then_inc(ktok_ready, 1)

            def outs(n, j):
                act.wait_ge(pe_ot, 2 * n + j + 1)
                after(act, pe_y, n)
                nc.scalar.activation(ogt[:, 4 * j:4 * j + 4, :], ps_t[:].rearrange("p (a s) -> p a s", s=P),
                                     ACT.Copy).then_inc(ogt_ready, 1)

            def half(r, b, first, ahead):
                n = 2 * r + b
                if not first:
                    outs(n - 1, 1)
                if b == 0:
                    values(n + 1, 1, 0)
                    keys(n, 0)
                    values(n + 1, 1, 1)
                    keys(n, 1)
                    gates(n + 1, 1, 0)
                    gates(n + 1, 1, 1)
                    outs(n, 0)
                    return
                keys(n, 0)
                keys(n, 1)
                if ahead:
                    for f in range(7):
                        exps(r + 1, f)
                outs(n, 0)
                if ahead:
                    exps(r + 1, 7)
                    for j in range(2):
                        values(n + 1, 0, j)
                    for j in range(2):
                        gates(n + 1, 0, j)

            weights(0)
            weights(1)
            for i in range(GROUPS):
                exps(0, 2 * i)
                exps(0, 2 * i + 1)
                weights(i + 2)
            weights(6)
            weights(7)
            act.wait_ge(ones_set, 2)
            for j in range(2):
                values(0, 0, j)
            for j in range(2):
                gates(0, 0, j)
            half(0, 0, True, True)
            half(0, 1, False, True)
            with act.Fori(1, NR - 1) as r:
                for b in range(B):
                    half(r, b, False, True)
            for b in range(B):
                half(NR - 1, b, False, False)
            outs(NH - 1, 1)

            def fetch(t):
                k, i = t.k, t.slot2
                after(act, pe_h, 2 * k - 3)
                after(act, hid_ready[0], k - 1)
                e = act.value_load(expert[0:1, 0, bass.ds(k, 1)], min_val=0, max_val=E - 1)
                nc.scalar.activation(b1_now[i][0][:], b1_tab[:, bass.ds(e, 1), :].rearrange("p o f -> p (o f)"), ACT.Copy)
                nc.scalar.activation(w1_now[i][0][:], w1_tab[:, bass.ds(e, 1), :].rearrange("p o f -> p (o f)"),
                                     ACT.Copy).then_inc(w1_now_ready[0], 1)

            def turned(t):
                k = t.k
                act.wait_ge(xg_turned, k + 1)
                after(act, pe_h, 2 * k - 2)
                nc.scalar.activation(xgt[t.slot2][:], ps_t[:, 0:P], ACT.Copy).then_inc(xgt_ready, 1)

            def hidden(t):
                k, i = t.k, t.slot2
                act.wait_ge(w1_now_ready[0], k + 1)
                after(act, pe_f, 2 * k - 3)
                act.wait_ge(pe_h, 2 * k + 1)
                for f in range(FB):
                    cols = slice(f * P, f * P + P)
                    last = nc.scalar.activation(hid[i][0][:, cols], ps_p[0][:, cols], ACT.Relu, bias=b1_now[i][0][:, f:f + 1])
                last.then_inc(hid_ready[0], 1)

            def body(t):
                if t.plus(1).exists():
                    turned(t.plus(1))
                    fetch(t.plus(1))
                hidden(t)

            act.wait_ge(experts_ready, 1)
            act.wait_ge(b1_ready, 1)
            act.wait_ge(w1_in, 16)
            fetch(Tile(0, 0))
            turned(Tile(0, 0))
            tile_loop(act, body)

        @block.vector
        def _(dve):
            def split_x(r):
                dve.wait_ge(pe_xt, r + 1)
                turned = ps_m[:, P:(B + 1) * P].rearrange("p (b t) -> p b t", b=B)
                nc.vector.tensor_copy(xt_hi[:], turned).then_inc(xt_half, 1)
                dve.wait_ge(xt_half, r + 1)
                nc.vector.tensor_tensor(xt_lo[:], turned, xt_hi[:].bitcast(F32), ALU.subtract).then_inc(xt_ready, 1)

            def rows(r, f):
                dve.wait_ge(exp_done, 8 * r + f + 1)
                nc.vector.scalar_tensor_tensor(qk[:, f, :, :, :].rearrange("p a b t -> p (a b t)"), expo[f % 2][:], 1.0,
                                               relu[f % 2][:], ALU.min, ALU.add).then_inc(qk_ready, 1)

            def mask(n, g):
                dve.wait_ge(pe_s, 4 * n + g + 1)
                after(dve, pe_o, 4 * n + g - 1)
                for i in range(2):
                    last = nc.vector.tensor_tensor(probs[g % 2][:, i::2, :], ps_s[i][:, 0:2 * P].rearrange("p (h t) -> p h t", t=P),
                                                   causal[:].unsqueeze(1).broadcast_to([P, 2, P]), ALU.mult)
                last.then_inc(probs_ready, 1)

            def numerator(n, b, g):
                i = 4 * n + g
                heads = ps_o[g % 2][:, 0:4 * VW].rearrange("p (h d) -> p h d", d=VW)
                dve.wait_ge(pe_o, i + 1)
                after(dve, og_ready, i - 1)
                nc.vector.tensor_scalar(den[g % 2][:], heads[:, :, HD:VW], 2.0, 2 * DEN_EPS, ALU.mult, ALU.add).then_inc(den_ready, 1)
                dve.wait_ge(den_ready, i + 1)
                nc.vector.reciprocal(rden[g % 2][:], den[g % 2][:]).then_inc(rden_ready, 1)
                dve.wait_ge(gate_ready, 2 * n + g // 2 + 1)
                nc.vector.scalar_tensor_tensor(num[g % 2][:], gate[b][:, 4 * g:4 * g + 4, :], 1.0,
                                               heads[:, :, 0:HD], ALU.add, ALU.mult).then_inc(num_ready, 1)

            def add_state(n, b, i, first):
                a, k = KV_LOTS[i]
                dve.wait_ge(pe_kv, 3 * n + i + 1)
                if first:
                    dve.wait_ge(zeroed, 2)
                else:
                    dve.wait_ge(state_ready, 3 * n + i - 5)
                for h, part in enumerate((slice(0, HD), slice(HD, P))):
                    lot = state[b][part, a:a + k, h, :]
                    new = ps_t[part, 0:2 * VW * k].rearrange("p (a h d) -> p a h d", h=2, d=VW)[:, :, h, :]
                    if first:
                        last = nc.vector.tensor_copy(lot, new)
                    else:
                        last = nc.vector.tensor_tensor(lot, new, lot, ALU.add)
                last.then_inc(state_ready, 1)

            def norm(r, b):
                n = 2 * r + b
                dve.wait_ge(pe_y, n + 1)
                dve.wait_ge(x_res_sem[b], 16 * r + 16)
                nc.vector.tensor_tensor(z[:], ps_m[:, 0:P], x_res[b][:], ALU.add).then_inc(z_ready, 1)
                dve.wait_ge(z_ready, n + 1)
                nc.vector.bn_stats(stats[:], z[:]).then_inc(stats_ready, 1)
                dve.wait_ge(consts, 1)
                dve.wait_ge(stats_ready, n + 1)
                nc.vector.bn_aggr(mv[:], stats[:]).then_inc(mv_ready, 1)
                dve.wait_ge(rstd_ready, n + 1)
                nc.vector.tensor_scalar(x1[:, n, :], z[:], mv[:, 0:1], rstd[:, 0:1], ALU.subtract, ALU.mult).then_inc(x1_ready, 1)

            def half(r, b, first, ahead):
                n = 2 * r + b
                start = first and b == 0
                project = ahead and b == 1
                mask(n, 0)
                mask(n, 1)
                if not start:
                    norm(r - 1 + b, 1 - b)
                numerator(n, b, 0)
                if project:
                    rows(r + 1, 0)
                mask(n, 2)
                numerator(n, b, 1)
                if project:
                    rows(r + 1, 1)
                add_state(n, b, 0, first)
                mask(n, 3)
                if project:
                    rows(r + 1, 2)
                numerator(n, b, 2)
                if project:
                    rows(r + 1, 3)
                add_state(n, b, 1, first)
                if project:
                    rows(r + 1, 4)
                numerator(n, b, 3)
                if project:
                    rows(r + 1, 5)
                add_state(n, b, 2, first)
                if project:
                    rows(r + 1, 6)
                    rows(r + 1, 7)
                if ahead and b == 0:
                    split_x(r + 1)

            def low_weights(i):
                dve.wait_ge(w_hi_ready, i + 1)
                nc.vector.tensor_tensor(w_lo[:, i, :], w_full[:, i, :], w_hi[:, i, :].bitcast(F32), ALU.subtract).then_inc(w_ready, 1)

            dve.wait_ge(consts, 2)
            split_x(0)
            low_weights(0)
            low_weights(1)
            for i in range(GROUPS):
                rows(0, 2 * i)
                rows(0, 2 * i + 1)
                low_weights(i + 2)
            low_weights(6)
            low_weights(7)
            for b in range(B):
                half(0, b, True, True)
            with dve.Fori(1, NR - 1) as r:
                for b in range(B):
                    half(r, b, False, True)
            for b in range(B):
                half(NR - 1, b, False, False)
            norm(NR - 1, 1)

            steps = [0]

            def then(ins):
                steps[0] += 1
                ins.then_inc(route, 1)
                dve.wait_ge(route, steps[0])

            v = nc.vector
            dve.wait_ge(x1_ready, NH)
            dve.wait_ge(route_consts, 5 + B)
            s, a, whole, up, sign, h, place, row = (t[:] for t in rt)
            then(v.tensor_tensor(s, x1[:, :, 0], x1[:, :, 1], ALU.add))
            then(v.scalar_tensor_tensor(a, s, -1.0, s, ALU.mult, ALU.max))
            then(v.tensor_copy(rt_int[:], a))
            then(v.tensor_copy(whole, rt_int[:]))
            then(v.tensor_tensor(up, whole, a, ALU.is_gt))
            then(v.tensor_tensor(whole, whole, up, ALU.subtract))
            then(v.tensor_scalar(sign, s, 0.0, -2.0, ALU.is_lt, ALU.mult))
            then(v.scalar_tensor_tensor(h, sign, 1.0, whole, ALU.add, ALU.mult))
            then(v.tensor_scalar(rt_int[:], h, float(WRAP), None, ALU.add))
            then(v.tensor_scalar(rt_low[:], rt_int[:], E - 1, None, ALU.bitwise_and))
            then(v.tensor_copy(h, rt_low[:]))
            v.tensor_tensor(onehot[:], h.unsqueeze(2).broadcast_to([P, NH, E]),
                            iota_e[:].unsqueeze(1).broadcast_to([P, NH, E]), ALU.is_equal).then_inc(onehot_ready, 1)
            then(v.tensor_tensor(lower_e[:], iota_e[:].unsqueeze(2).broadcast_to([P, E, E]),
                                 iota_e[:].unsqueeze(1).broadcast_to([P, E, E]), ALU.is_gt))
            dve.wait_ge(ranked, 1)
            then(v.tensor_tensor(over[:], ps_s[1][:, 0:E].unsqueeze(2).broadcast_to([P, E, NH]),
                                 iota_k[:, 0:NH].unsqueeze(1).broadcast_to([P, E, NH]), ALU.is_gt))
            then(v.tensor_reduce(tiles_of[:], over[:], AX.X, ALU.add))
            then(v.tensor_tensor(low_prod[:], lower_e[:], tiles_of[:].unsqueeze(1).broadcast_to([P, E, E]), ALU.mult))
            then(v.tensor_reduce(tot[:], low_prod[:], AX.X, ALU.add))
            then(v.tensor_scalar(first_tile[:], tot[:], float(P), None, ALU.mult))
            then(v.tensor_tensor(place3[:], ps_s[0][:, 0:NH * E].rearrange("p (n e) -> p n e", e=E),
                                 first_tile[:].unsqueeze(1).broadcast_to([P, NH, E]), ALU.add))
            then(v.tensor_tensor(place4[:], place3[:], onehot[:], ALU.mult))
            then(v.tensor_reduce(place, place4[:], AX.X, ALU.add))
            then(v.tensor_copy(rt_int[:], place))
            then(v.tensor_scalar(rt_low[:], rt_int[:], P - 1, None, ALU.bitwise_and))
            then(v.tensor_copy(row, rt_low[:]))
            then(v.tensor_tensor(place, place, row, ALU.subtract))
            then(v.tensor_tensor(at_tile[:, :, 0, :], place.unsqueeze(2).broadcast_to([P, NH, TILES]),
                                 iota_k[:].unsqueeze(1).broadcast_to([P, NH, TILES]), ALU.is_equal))
            v.tensor_scalar(at_tile[:, :, 1, :], at_tile[:, :, 0, :], row_no[:, 0:1], None, ALU.mult)
            v.tensor_tensor(at_tile[:, :, 2, :], at_tile[:, :, 0, :], iota_c[:].broadcast_to([P, NH, TILES]), ALU.mult)
            for n in range(NH):
                last = v.tensor_scalar(at_row[:, n, :], iota_p[:], row[:, n:n + 1], None, ALU.is_equal)
            last.then_inc(places_ready, 1)
            then(v.tensor_tensor(reached[:], iota_k[:].unsqueeze(2).broadcast_to([P, TILES, E]),
                                 first_tile[:].unsqueeze(1).broadcast_to([P, TILES, E]), ALU.is_ge))
            then(v.tensor_reduce(exp_f[:], reached[:], AX.X, ALU.add))
            then(v.tensor_copy(reached_int[:], exp_f[:]))
            then(v.tensor_scalar(expert[:, 0, :], exp_f[:], -1.0, None, ALU.add))
            v.tensor_scalar(expert[:, 1, :], reached_int[:], E - 1, None, ALU.bitwise_and).then_inc(experts_ready, 1)
            dve.wait_ge(listed, 1)
            then(v.tensor_copy(found[:].rearrange("p a k -> p (a k)"), ps_m[:, 0:3 * TILES]))
            then(v.scalar_tensor_tensor(idx_f[:], found[:, 2, :], float(P), found[:, 1, :], ALU.mult, ALU.add))
            v.tensor_copy(idx_from[:], idx_f[:]).then_inc(indices_ready, 1)
            then(v.tensor_scalar(gaps[:], found[:, 0, :], -float(NOWHERE), float(NOWHERE), ALU.mult, ALU.add))
            then(v.tensor_tensor(gaps[:], gaps[:], idx_f[:], ALU.add))
            v.tensor_copy(idx_to[:], gaps[:]).then_inc(indices_ready, 1)
            dve.wait_ge(b1_turned, 1)
            v.tensor_copy(b1_tab[:].rearrange("p e f -> p (e f)"), ps_o[0][:, 0:E * FB]).then_inc(b1_ready, 1)
            dve.wait_ge(b1_ready, 1)
            dve.wait_ge(b2_ready, 1)
            dve.wait_ge(w1_in, 16)
            dve.wait_ge(experts_ready, 1)

            def take(t):
                k, i = t.k, t.slot2
                after(dve, pe_h, 2 * k - 2)
                after(dve, hid_ready[1], k - 1)
                e = dve.value_load(expert[0:1, 1, bass.ds(k, 1)], min_val=0, max_val=E - 1)
                v.tensor_copy(b1_now[i][1][:], b1_tab[:, bass.ds(e, 1), :].rearrange("p o f -> p (o f)"))
                v.tensor_copy(w1_now[i][1][:], w1_tab[:, bass.ds(e, 1), :].rearrange("p o f -> p (o f)"))\
                    .then_inc(w1_now_ready[1], 1)
                return e

            def keep(t, e):
                dve.wait_ge(xg_in[t.slot4], 16 * t.turn4 + 16)
                after(dve, z2_ready, t.k - 1)
                v.tensor_tensor(xg_res[t.slot2][:], xg[t.slot4][:], b2_tab[:, bass.ds(e, 1), :].rearrange("p o d -> p (o d)"),
                                ALU.add).then_inc(xg_kept, 1)

            def hidden(t):
                k, i = t.k, t.slot2
                dve.wait_ge(w1_now_ready[1], k + 1)
                after(dve, pe_f, 2 * k - 2)
                dve.wait_ge(pe_h, 2 * k + 2)
                for f in range(FB):
                    cols = slice(f * P, f * P + P)
                    last = v.tensor_scalar(hid[i][1][:, cols], ps_p[1][:, cols], b1_now[i][1][:, f:f + 1], 0.0, ALU.add, ALU.max)
                last.then_inc(hid_ready[1], 1)

            def moments(t):
                k, i = t.k, t.slot2
                dve.wait_ge(pe_f, 2 * k + 2)
                dve.wait_ge(xg_kept, k + 1)
                after(dve, y2_ready, k)
                v.scalar_tensor_tensor(z2[:], ps_o[i][:, 0:P], 0.5, xg_res[i][:], ALU.mult, ALU.add).then_inc(z2_ready, 1)
                dve.wait_ge(z2_ready, k + 1)
                v.bn_stats(stats[:], z2[:]).then_inc(stats2_ready, 1)
                dve.wait_ge(experts_ready, 1)
                dve.wait_ge(stats2_ready, k + 1)
                v.bn_aggr(mv[:], stats[:]).then_inc(mv2_ready, 1)

            def finish(t):
                k, i = t.k, t.slot2
                dve.wait_ge(rstd2_ready, k + 1)
                after(dve, y2_out[i], 16 * t.turn2)
                v.tensor_scalar(y2[i][:], z2[:], mv[:, 0:1], rstd[:, 0:1], ALU.subtract, ALU.mult).then_inc(y2_ready, 1)

            def body(t):
                if t.plus(-2).exists():
                    finish(t.plus(-2))
                if t.plus(1).exists():
                    e = take(t.plus(1))
                hidden(t)
                if t.plus(-1).exists():
                    moments(t.plus(-1))
                if t.plus(1).exists():
                    keep(t.plus(1), e)

            keep(Tile(0, 0), take(Tile(0, 0)))
            tile_loop(dve, body)
            finish(Tile(0, TILES - 2))
            moments(Tile(0, TILES - 1))
            finish(Tile(0, TILES - 1))

        @block.tensor
        def _(pe):
            def turn_x(r):
                pe.wait_ge(x_in_sem, 16 * r + 16)
                after(pe, z_ready, 2 * r - 2)
                for b in range(B):
                    last = nc.tensor.transpose(ps_m[:, (b + 1) * P:(b + 2) * P], x_in[:, b, :], ident[:])
                last.then_inc(pe_xt, 1)

            def three(dst, pairs):
                for i, (lhs, rhs) in enumerate(pairs):
                    last = nc.tensor.matmul(dst, lhs, rhs, start=(i == 0), stop=(i == 2))
                return last

            def project_qk(r, f):
                if f == 0:
                    pe.wait_ge(xt_ready, r + 1)
                if f < 2:
                    after(pe, gate_ready, 4 * r - 1 + f)
                else:
                    pe.wait_ge(exp_done, 8 * r + f - 1)
                rows = [t[:].rearrange("p b t -> p (b t)") for t in (xt_hi, xt_lo)]
                for i in range(2):
                    cols = slice(256 * i + P * (f % 2), 256 * i + P * (f % 2) + P)
                    hi, lo = w_hi[:, f // 2, cols], w_lo[:, f // 2, cols]
                    last = three(ps_p[f % 2][:, 256 * i:256 * i + 256], [(hi, rows[0]), (hi, rows[1]), (lo, rows[0])])
                last.then_inc(pe_qk, 1)

            def project_vg(r, b, i):
                m, j = 2 * r + b, i % 2
                if i >= 2:
                    pe.wait_ge(v_ready, 2 * m + 1 + j)
                elif b == 0:
                    pe.wait_ge(exp_done, 8 * r + 7 + j)
                else:
                    pe.wait_ge(gate_ready, 4 * r + 1 + j)
                hi, lo = w_hi[:, 4 + i, :], w_lo[:, 4 + i, :]
                three(ps_p[j][:], [(xt_hi[:, b, :], hi), (xt_hi[:, b, :], lo), (xt_lo[:, b, :], hi)])\
                    .then_inc(pe_v if i < 2 else pe_g, 1)

            def scores(r, b, g):
                n = 2 * r + b
                pe.wait_ge(qk_ready, 8 * r + 2 * g + 2)
                after(pe, probs_ready, 4 * n + g)
                for a in range(2):
                    for h, part in enumerate((slice(0, HD), slice(HD, P))):
                        last = nc.tensor.matmul(ps_s[h][:, a * P:a * P + P], qk[part, 2 * g + a, 1, b, :],
                                                qk[part, 2 * g + a, 0, b, :], start=True, stop=True)
                last.then_inc(pe_s, 1)

            def turn_k(n, b, j):
                after(pe, *((ogt_ready, 2 * n) if j == 0 else (ktok_ready, 2 * n + 1)))
                for i in range(4):
                    last = nc.tensor.transpose(ps_t[:, i * P:i * P + P], qk[:, 4 * j + i, 1, b, :], ident[:])
                last.then_inc(pe_kt, 1)

            def attend(n, b, g, first):
                after(pe, num_ready, 4 * n + g - 1)
                pe.wait_ge(v_ready, 2 * n + g // 2 + 1)
                if not first:
                    pe.wait_ge(state_ready, 3 * n - 3)
                pe.wait_ge(probs_ready, 4 * n + g + 1)
                for a in range(2):
                    if not first:
                        nc.tensor.matmul(ps_o[g % 2][:, 2 * VW * a:2 * VW * (a + 1)], qk[:, 2 * g + a, 0, b, :],
                                         state[b][:, 2 * g + a, :, :].rearrange("p h d -> p (h d)"), start=True, stop=False,
                                         skip_group_check=True)
                    for i in range(2 * a, 2 * a + 2):
                        last = nc.tensor.matmul(ps_o[g % 2][:, i * VW:i * VW + VW], probs[g % 2][:, i, :], v1[b][:, 4 * g + i, :],
                                                start=first, stop=True, skip_group_check=True)
                last.then_inc(pe_o, 1)

            def sum_kv(n, b, i):
                a, k = KV_LOTS[i]
                if i == 0:
                    pe.wait_ge(ktok_ready, 2 * n + 2)
                    pe.wait_ge(v_ready, 2 * n + 2)
                else:
                    pe.wait_ge(state_ready, 3 * n + i)
                for j in range(k):
                    last = nc.tensor.matmul(ps_t[:, 2 * VW * j:2 * VW * (j + 1)], ktok[:, a + j, :],
                                            v1[b][:, 2 * (a + j):2 * (a + j) + 2, :].rearrange("p h d -> p (h d)"),
                                            start=True, stop=True)
                last.then_inc(pe_kv, 1)

            def turn_o(n, j):
                pe.wait_ge(og_ready, 4 * n + 2 * j + 2)
                pe.wait_ge(*((state_ready, 3 * n + 3) if j == 0 else (ogt_ready, 2 * n + 1)))
                for i in range(4):
                    a = 4 * j + i
                    last = nc.tensor.transpose(ps_t[:, i * P:i * P + P],
                                               og[:, 2 * a:2 * a + 2, :].rearrange("p h d -> p (h d)"), ident[:])
                last.then_inc(pe_ot, 1)

            def project_out(r, b, ahead=True):
                n = 2 * r + b
                pe.wait_ge(ogt_ready, 2 * n + 2)
                if b == 0 and ahead:
                    pe.wait_ge(xt_ready, r + 2)
                else:
                    pe.wait_ge(z_ready, n)
                for a in range(PAIRS):
                    last = nc.tensor.matmul(ps_m[:, 0:P], ogt[:, a, :], wo[:, a, :], start=(a == 0), stop=(a == PAIRS - 1))
                last.then_inc(pe_y, 1)

            def half(r, b, first, ahead):
                n = 2 * r + b
                start = first and b == 0
                project = ahead and b == 1
                scores(r, b, 0)
                if not start:
                    turn_o(n - 1, 1)
                if b == 0:
                    project_vg(r, 1, 0)
                turn_k(n, b, 0)
                scores(r, b, 1)
                if not start:
                    project_out(r - 1 + b, 1 - b, ahead)
                if b == 0:
                    project_vg(r, 1, 1)
                turn_k(n, b, 1)
                attend(n, b, 0, first)
                if project:
                    project_qk(r + 1, 0)
                scores(r, b, 2)
                if project:
                    project_qk(r + 1, 1)
                attend(n, b, 1, first)
                sum_kv(n, b, 0)
                project_qk(r + 1, 2) if project else b or project_vg(r, 1, 2)
                scores(r, b, 3)
                attend(n, b, 2, first)
                if project:
                    project_qk(r + 1, 3)
                sum_kv(n, b, 1)
                project_qk(r + 1, 4) if project else b or project_vg(r, 1, 3)
                attend(n, b, 3, first)
                if project:
                    project_qk(r + 1, 5)
                sum_kv(n, b, 2)
                if project:
                    project_qk(r + 1, 6)
                if ahead and b == 0:
                    turn_x(r + 1)
                turn_o(n, 0)
                if project:
                    project_qk(r + 1, 7)
                    for i in range(4):
                        project_vg(r + 1, 0, i)

            pe.wait_ge(consts, 1)
            turn_x(0)
            for f in range(PAIRS):
                pe.wait_ge(w_ready, f // 2 + 1)
                project_qk(0, f)
            for i in range(4):
                pe.wait_ge(w_ready, 5 + i)
                project_vg(0, 0, i)
            pe.wait_ge(wo_in, 16)
            for b in range(B):
                half(0, b, True, True)
            with pe.Fori(1, NR - 1) as r:
                for b in range(B):
                    half(r, b, False, True)
            for b in range(B):
                half(NR - 1, b, False, False)
            turn_o(NH - 1, 1)
            project_out(NR - 1, 1)

            pe.wait_ge(b1_in, 16)
            nc.tensor.transpose(ps_o[0][:, 0:E * FB], b1_rows[:], ident[0:E * FB, 0:E * FB]).then_inc(b1_turned, 1)
            pe.wait_ge(onehot_ready, 1)
            rows = onehot[:].rearrange("p n e -> p (n e)")
            nc.tensor.matmul(ps_s[0][:, 0:NH * E], before[:], rows, start=True, stop=False, skip_group_check=True)
            for d in range(1, NH):
                nc.tensor.matmul(ps_s[0][:, d * E:NH * E], ones_bf[:], rows[:, 0:(NH - d) * E], start=False, stop=(d == NH - 1),
                                 skip_group_check=True)
            for n in range(NH):
                last = nc.tensor.matmul(ps_s[1][:, 0:E], ones_bf[:], onehot[:, n, :], start=(n == 0), stop=(n == NH - 1))
            last.then_inc(ranked, 1)
            pe.wait_ge(places_ready, 1)
            for n in range(NH):
                last = nc.tensor.matmul(ps_m[:, 0:3 * TILES], at_row[:, n, :], at_tile[:, n, :, :].rearrange("p a k -> p (a k)"),
                                        start=(n == 0), stop=(n == NH - 1))
            last.then_inc(listed, 1)

            def turn_rows(t):
                pe.wait_ge(xg_in[t.slot4], 16 * t.turn4 + 16)
                after(pe, xgt_ready, t.k)
                nc.tensor.transpose(ps_t[:, 0:P], xg[t.slot4][:], ident[:]).then_inc(xg_turned, 1)

            def into_hidden(t, j):
                k, i = t.k, t.slot2
                pe.wait_ge(xgt_ready, k + 1)
                pe.wait_ge(w1_now_ready[j], k + 1)
                after(pe, hid_ready[j], k)
                for f in range(FB):
                    last = nc.tensor.matmul(ps_p[j][:, f * P:f * P + P], w1_now[i][j][:, f * P:f * P + P], xgt[i][:],
                                            start=True, stop=True)
                last.then_inc(pe_h, 1)

            def out_of_hidden(t, j, e):
                k, i = t.k, t.slot2
                if j == 0:
                    after(pe, z2_ready, k - 1)
                pe.wait_ge(hid_ready[j], k + 1)
                for f in range(FB):
                    nc_last = nc.tensor.matmul(ps_o[i][:, 0:P], hid[i][j][:, f * P:f * P + P],
                                               w2_tab[:, bass.ds(e, 1), f, :].rearrange("p o d -> p (o d)"),
                                               start=(j == 0 and f == 0), stop=(j == 1 and f == FB - 1))
                nc_last.then_inc(pe_f, 1)

            def experts_of(k):
                return [pe.value_load(expert[0:1, j, bass.ds(k, 1)], min_val=0, max_val=E - 1) for j in range(2)]

            def body(t):
                before_it = t.plus(-1)
                pair = experts_of(before_it.k) if before_it.exists() else None
                if t.plus(1).exists():
                    turn_rows(t.plus(1))
                for j in range(2):
                    into_hidden(t, j)
                    if pair:
                        out_of_hidden(before_it, j, pair[j])

            pe.wait_ge(experts_ready, 1)
            pe.wait_ge(w2_in, 16)
            pe.wait_ge(b1_ready, 1)
            turn_rows(Tile(0, 0))
            tile_loop(pe, body)
            pair = experts_of(TILES - 1)
            for j in range(2):
                out_of_hidden(Tile(0, TILES - 1), j, pair[j])


_INS = ["L0_attn_x", "L0_attn_w_qkv", "L0_attn_w_gate", "L0_attn_w_out",
        "L0_ffn_W1", "L0_ffn_b1", "L0_ffn_W2", "L0_ffn_b2"]
_OUTS = [((2, 1024, 128), "float32")]


def kernel(**inputs):
    import numpy as _np
    import concourse.bacc as _bacc
    from concourse import mybir as _mybir
    from concourse.bass_utils import run_bass_kernel_spmd as _run

    nc = _bacc.Bacc("TRN2", target_bir_lowering=False, num_devices=1)
    arrays, args = {}, []
    for name in _INS:
        a = _np.ascontiguousarray(inputs[name])
        arrays[f"in_{name}_dram"] = a
        args.append(nc.dram_tensor(f"in_{name}_dram", a.shape, _mybir.dt.from_np(a.dtype), kind="ExternalInput").ap())
    for i, (shape, dtype) in enumerate(_OUTS):
        dt = _mybir.dt.from_np(_np.dtype(dtype))
        args.append(nc.dram_tensor(f"out_{i}_dram", shape, dt, kind="ExternalOutput").ap())
    build(nc, *args)
    r = _run(nc, [arrays], core_ids=[0])
    got = tuple(r.results[0][f"out_{i}_dram"] for i in range(len(_OUTS)))
    return got[0]
```

```python
from contextlib import ExitStack

import concourse.bass as bass
from concourse import mybir

F32 = mybir.dt.float32
F32R = mybir.dt.float32r
BF16 = mybir.dt.bfloat16
I32 = mybir.dt.int32
ALU = mybir.AluOpType
ACT = mybir.ActivationFunctionType
AX = mybir.AxisListType

P = 128
HEADS, HD = 16, 64
PAIRS = HEADS // 2
GROUPS = HEADS // 4
VW = HD + 1
LN_EPS = 1e-5
DEN_EPS = 1e-6


def build(nc, x, w_qkv, w_gate, w_out, ffn_w1, ffn_b1, ffn_w2, ffn_b2, out):
    B, T, D = x.shape
    NR = T // P
    NH = B * NR
    HDALL = HEADS * HD
    E, _, F = ffn_w1.shape
    FB = F // P
    TILES = NH
    JOBS = 2 * TILES + E - 1
    LAG = E // 2
    SEATS = 2 * E
    PLANNED = (JOBS + 1) // 2
    assert D == P and E & (E - 1) == 0 and B == 2
    LOTS = E // 2 * B * T
    lots = nc.dram_tensor("lots", (LOTS, D + 1), F32).ap()
    out_rows = out.rearrange("b t d -> (b t) d")

    with ExitStack() as ctx:
        def sb(name, shape, dt=F32):
            return ctx.enter_context(nc.sbuf_tensor(name, shape, dt))

        def pb(name):
            return ctx.enter_context(nc.psum_tensor(name, [P, 512], F32))

        def sem(name):
            return ctx.enter_context(nc.semaphore(name))

        ident = sb("ident", [P, P])
        causal = sb("causal", [P, P])
        w_full = sb("w_full", [P, 8, 512])
        w_hi = sb("w_hi", [P, 8, 512], F32R)
        w_lo = sb("w_lo", [P, 8, 512], F32R)
        wo = sb("wo", [P, PAIRS, P])
        x_in = sb("x_in", [P, B, P])
        x_res = [sb(f"x_res{b}", [P, P]) for b in range(B)]
        xt_hi = sb("xt_hi", [P, B, P], F32R)
        xt_lo = sb("xt_lo", [P, B, P], F32R)
        expo = [sb(f"expo{i}", [P, 512]) for i in range(2)]
        relu = [sb(f"relu{i}", [P, 512]) for i in range(2)]
        qk = sb("qk", [P, PAIRS, 2, B, P])
        ktok = sb("ktok", [P, PAIRS, P])
        v1 = [sb(f"v1_{b}", [P, HEADS, VW]) for b in range(B)]
        gate = [sb(f"gate{b}", [P, HEADS, HD]) for b in range(B)]
        probs = [sb(f"probs{i}", [P, 4, P]) for i in range(2)]
        den = [sb(f"den{i}", [P, 4, 1]) for i in range(2)]
        rden = [sb(f"rden{i}", [P, 4, 1]) for i in range(2)]
        num = [sb(f"num{i}", [P, 4, HD]) for i in range(2)]
        og = sb("og", [P, HEADS, HD])
        ogt = sb("ogt", [P, PAIRS, P])
        state = [sb(f"state{b}", [P, PAIRS, 2, VW]) for b in range(B)]
        z = sb("z", [P, P])
        stats = sb("stats", [P, 6])
        mv = sb("mv", [P, 2])
        rstd = sb("rstd", [P, 1])
        veps = sb("veps", [P, 1])
        eps = sb("eps", [P, 1])
        minus_half = sb("minus_half", [P, 1])
        x1 = [sb(f"x1_{b}", [P, D + 1]) for b in range(B)]

        w1_tab = sb("w1_tab", [P, E, F])
        w2_tab = sb("w2_tab", [P, E, FB, D])
        b1_rows = sb("b1_rows", [E * FB, P])
        b1_tab = sb("b1_tab", [P, E, FB])
        b2_rows = sb("b2_rows", [P, D])
        b2_by_tile = w_full[:, 0:4, :].rearrange("p a (b d) -> p (a b) d", d=D)
        bias_all = w_full[:, 4:8, :].rearrange("p a (b d) -> p (a b) d", d=D)
        expert_weight = sb("expert_weight", [P, TILES, E])
        expert_weight_t = sb("expert_weight_t", [P, P])

        before = sb("before", [P, P], BF16)
        ones_bf = sb("ones_bf", [P, P], BF16)
        iota_e = sb("iota_e", [P, E])
        row_no = sb("row_no", [P, NH, 1])
        place_no = sb("place_no", [P, TILES])
        edge_no = sb("edge_no", [P, 2, TILES])
        job_no = sb("job_no", [P, 1])
        way = sb("way", [P, E])
        signed = sb("signed", [P, E], BF16)
        lot_start = sb("lot_start", [P, E])
        seat_no = sb("seat_no", [P, SEATS])
        up_to_e = sb("up_to_e", [P, E, E])
        lower_t = sb("lower_t", [P, TILES, TILES])
        rt_sum, rt_abs, rt_whole, rt_sign = (sb(f"rt_{s}", [P, 1]) for s in ("sum", "abs", "whole", "sign"))
        rt_int, rt_signed, rt_low = (sb(f"rt_{s}", [P, 1], I32) for s in ("int", "signed", "low"))
        onehot = sb("onehot", [P, E], BF16)
        seen = sb("seen", [P, E])
        spot = sb("spot", [P, E])
        spot_own = sb("spot_own", [P, E])
        place_f = sb("place_f", [P, 1])
        place = [sb(f"place{b}", [P, 1], I32) for b in range(B)]

        count = sb("count", [P, E])
        span, first, first_way, origin = (sb(s, [P, E]) for s in ("span", "first", "first_way", "origin"))
        part_e = sb("part_e", [P, E, E])
        end = sb("end", [P, E])
        past_end = sb("past_end", [P, TILES, E])
        own, own_way, own_origin = (sb(s, [P, TILES, E]) for s in ("own", "own_way", "own_origin"))
        row_way, row_origin, along = (sb(s, [P, TILES]) for s in ("row_way", "row_origin", "along"))
        idx_from = sb("idx_from", [P, TILES], I32)
        group = sb("group", [P, TILES])
        past_edge = sb("past_edge", [P, 2, TILES, E])
        edge = sb("edge", [P, 2, TILES])
        jobs_of = sb("jobs_of", [P, TILES])
        part_t = sb("part_t", [P, TILES, TILES])
        first_job = sb("first_job", [P, TILES])
        turn = sb("turn", [P, TILES])
        past_job, turned_by = sb("past_job", [P, TILES]), sb("turned_by", [P, TILES])
        job_tile, job_turn, job_seat = (sb(f"job_{s}", [P, 1]) for s in ("tile", "turn", "seat"))
        job_seat_int, job_low = sb("job_seat_int", [P, 1], I32), sb("job_low", [P, 1], I32)
        job_plan = sb("job_plan", [P, 3])
        plan = sb("plan", [1, 3, 2 * PLANNED])
        pe_words = sb("pe_words", [1, PLANNED + 1, 4], I32)
        act_words, dve_words = sb("act_words", [1, PLANNED, 4], I32), sb("dve_words", [1, PLANNED, 4], I32)
        from_seat = sb("from_seat", [P, TILES, SEATS])
        near = sb("near", [P, TILES, SEATS])
        weight = sb("weight", [P, TILES * SEATS + 1])

        idx_to = [sb(f"idx_to{i}", [P, 1], I32) for i in range(2)]
        idx_g = [sb(f"idx_g{i}", [P, 1], I32) for i in range(3)]
        xg = [sb(f"xg{i}", [P, P]) for i in range(2)]
        rows_all = sb("rows_all", [P, TILES, D + 1])
        acc = sb("acc", [P, TILES, P])
        xt_all = sb("xt_all", [P, TILES, P])
        w1_now = [sb(f"w1_now{i}", [P, F]) for i in range(4)]
        b1_now = [sb(f"b1_now{i}", [P, FB]) for i in range(4)]
        hid = [expo[0], expo[1], relu[0], relu[1]]
        y2 = [sb(f"y2_{i}", [P, P]) for i in range(2)]

        ps_p = [pb(f"ps_p{i}") for i in range(2)]
        ps_s = [pb(f"ps_s{i}") for i in range(2)]
        ps_o = [pb(f"ps_o{i}") for i in range(2)]
        ps_t = pb("ps_t")
        ps_m = pb("ps_m")

        w_in = [sem(f"w_in{i}") for i in range(8)]
        wo_in = sem("wo_in")
        x_in_sem = sem("x_in_sem")
        x_res_sem = [sem(f"x_res_sem{b}") for b in range(B)]
        consts = sem("consts")
        ones_set = sem("ones_set")
        route_fill, route_consts = sem("route_fill"), sem("route_consts")
        pool_consts = sem("pool_consts")
        veps_ready = sem("veps_ready")
        filled = sem("filled")
        w_hi_ready, w_hi_vg_ready = sem("w_hi_ready"), sem("w_hi_vg_ready")
        w_ready = sem("w_ready")
        pe_xt, xt_half, xt_ready = sem("pe_xt"), sem("xt_half"), sem("xt_ready")
        pe_qk, exp_done, qk_ready = sem("pe_qk"), sem("exp_done"), sem("qk_ready")
        pe_v, v_ready, pe_g, gate_ready = sem("pe_v"), sem("v_ready"), sem("pe_g"), sem("gate_ready")
        pe_s, probs_ready = sem("pe_s"), sem("probs_ready")
        pe_kt, ktok_ready = sem("pe_kt"), sem("ktok_ready")
        pe_o, den_ready, rden_ready, num_ready, og_ready = (
            sem("pe_o"), sem("den_ready"), sem("rden_ready"), sem("num_ready"), sem("og_ready"))
        pe_kv, state_ready = sem("pe_kv"), sem("state_ready")
        pe_ot, ogt_ready = sem("pe_ot"), sem("ogt_ready")
        pe_y, z_ready, stats_ready, mv_ready, rstd_ready, x1_ready = (
            sem("pe_y"), sem("z_ready"), sem("stats_ready"), sem("mv_ready"), sem("rstd_ready"), sem("x1_ready"))
        x1_out = [sem(f"x1_out{b}") for b in range(B)]
        w1_in, w2_in, b1_in, b2_in = sem("w1_in"), sem("w2_in"), sem("b1_in"), sem("b2_in")
        zeroed, rows_zeroed, lots_zeroed = sem("zeroed"), sem("rows_zeroed"), sem("lots_zeroed")
        b1_turned, b1_ready = sem("b1_turned"), sem("b1_ready")
        grouped, ranked, spotted, seen_ready, placed = (
            sem("grouped"), sem("ranked"), sem("spotted"), sem("seen_ready"), sem("placed"))
        planned, indices_ready = sem("planned"), sem("indices_ready")
        jobs_planned, plan_turned, plan_ready = sem("jobs_planned"), sem("plan_turned"), sem("plan_ready")
        idx_g_ready, rows_kept = sem("idx_g_ready"), sem("rows_kept")
        rows_in = [sem(f"rows_in{i}") for i in range(3)]
        rows_turned, xt_all_ready = sem("rows_turned"), sem("xt_all_ready")
        w1_now_ready, pe_h, pe_f = sem("w1_now_ready"), sem("pe_h"), sem("pe_f")
        hid_ready = [sem(f"hid_ready{i}") for i in range(2)]
        b2_spread, weights_set, weights_turned, weights_t_ready, bias_made, bias_ready, based, added = (
            sem("b2_spread"), sem("weights_set"), sem("weights_turned"), sem("weights_t_ready"), sem("bias_made"),
            sem("bias_ready"), sem("based"), sem("added"))
        stats2_ready, mv2_ready, veps2_ready, rstd2_ready, y2_ready, idx_to_ready = (
            sem("stats2_ready"), sem("mv2_ready"), sem("veps2_ready"), sem("rstd2_ready"), sem("y2_ready"), sem("idx_to_ready"))
        y2_out = [sem(f"y2_out{i}") for i in range(2)]

        block = ctx.enter_context(nc.Block())

        STAGES = 9
        RANKS = 2 * P
        bias_banks = (ps_s[1], ps_m)
        KV_LOTS = [(0, 3), (3, 3), (6, 2)]

        def after(eng, s, value):
            if not (isinstance(value, int) and value <= 0):
                eng.wait_ge(s, value)

        class Step:

            def __init__(self, i, c):
                self.i, self.c, self.u = i, c, 2 * i + c
                self.slot = c % 2

            def plus(self, d):
                return Step(self.i, self.c + d)

            def of_tile(self):
                return not isinstance(self.u, int) or 0 <= self.u < TILES

            def job(self, c):
                return Job(self, c)

        class Job:

            def __init__(self, step, c):
                self.j = 2 * step.u + c
                self.before = step.u + c // 2
                self.slot4, self.slot2 = (2 * step.c + c) % 4, c % 2

            def exists(self):
                return not isinstance(self.j, int) or 0 <= self.j < JOBS

        STEPS = PLANNED + 2

        def all_steps(eng, body):
            begin, end_ = LAG + 4, TILES - 2
            for u in range(begin):
                body(Step(0, u))
            with eng.Fori(0, (end_ - begin) // 2) as i:
                for c in range(2):
                    body(Step(i, begin + c))
            for u in range(end_, STEPS):
                body(Step(0, u))

        def wait_alone(eng, held, count, *waits):
            waits = [(s, value if isinstance(value, int) else eng.snap(eng.to_reg(value))) for s, value in waits]
            eng.wait_ge(held, count)
            for s, value in waits:
                after(eng, s, value)

        def load(eng, registers, words, tops):
            eng.load(registers, words)
            return [eng.snap(register, min_val=0, max_val=top) for register, top in zip(registers, tops)]

        @block.sync
        def _(sp):
            def load_x(r):
                sp.dma_start(x_in[:], x[:, bass.ts(r, P), :].rearrange("b p d -> p b d")).then_inc(x_in_sem, 16)

            def load_res(r, b):
                sp.dma_start(x_res[b][:], x[b, bass.ts(r, P), :]).then_inc(x_res_sem[b], 16)

            load_x(0)
            for g in range(GROUPS):
                for part in range(2):
                    sp.dma_start(w_full[:, g, 256 * part:256 * part + 256],
                                 w_qkv[:, HDALL * part + 256 * g:HDALL * part + 256 * g + 256]).then_inc(w_in[g], 16)
            for j in range(2):
                sp.dma_start(w_full[:, 4 + j, :], w_qkv[:, 2 * HDALL + 512 * j:2 * HDALL + 512 * j + 512]).then_inc(w_in[4 + j], 16)
            for j in range(2):
                sp.dma_start(w_full[:, 6 + j, :], w_gate[:, 512 * j:512 * j + 512]).then_inc(w_in[6 + j], 16)
            sp.wait_ge(pe_xt, 1)
            load_x(1)
            for b in range(B):
                load_res(0, b)
            sp.dma_start(wo[:], w_out.rearrange("(j p) d -> p j d", p=P)).then_inc(wo_in, 16)
            sp.dma_start(b1_rows[:], ffn_b1.rearrange("e (f p) -> (e f) p", p=P)).then_inc(b1_in, 16)
            sp.dma_start(b2_rows[:],
                         ffn_b2.rearrange("(o e) d -> o e d", o=1).broadcast_to([TILES, E, D])).then_inc(b2_in, 16)
            sp.dma_start(w1_tab[:], ffn_w1.rearrange("e p f -> p e f")).then_inc(w1_in, 16)
            sp.dma_start(w2_tab[:], ffn_w2.rearrange("e (f p) d -> p e f d", p=P)).then_inc(w2_in, 16)

            sp.wait_ge(rows_zeroed, 1)
            for q in range(E // 2):
                sp.dma_start(lots[bass.ts(q, B * T), :].rearrange("(p k) d -> p (k d)", p=P),
                             rows_all[:].rearrange("p k d -> p (k d)")).then_inc(lots_zeroed, 16)

            def rounds(r, ahead):
                if ahead:
                    sp.wait_ge(pe_xt, r + 2)
                    load_x(r + 2)
                for b in range(B):
                    sp.wait_ge(z_ready, 2 * r + b + 1)
                    load_res(r + 1, b)

            with sp.Fori(0, NR - 2) as r:
                rounds(r, True)
            rounds(NR - 2, False)
            for i in range(2):
                sp.wait_ge(y2_out[i], 16 * (TILES // 2))

        @block.gpsimd
        def _(pool):
            nc.gpsimd.memset(ident[:], 0.0).then_inc(filled, 1)
            nc.gpsimd.memset(causal[:], 1.0).then_inc(filled, 1)
            pool.wait_ge(filled, 2)
            nc.gpsimd.affine_select(out=ident[:], in_=ident[:], compare_op=ALU.not_equal, fill=1.0, base=0,
                                    pattern=[[-1, P]], channel_multiplier=1).then_inc(consts, 1)
            nc.gpsimd.affine_select(out=causal[:], in_=causal[:], compare_op=ALU.is_ge, fill=0.0, base=0,
                                    pattern=[[1, P]], channel_multiplier=-1).then_inc(consts, 1)
            nc.gpsimd.memset(eps[:], LN_EPS).then_inc(pool_consts, 1)
            nc.gpsimd.memset(minus_half[:], -0.5).then_inc(pool_consts, 1)
            for b in range(B):
                nc.gpsimd.memset(v1[b][:, :, HD:VW], 1.0).then_inc(ones_set, 1)
            for i in range(GROUPS, 2 * GROUPS):
                pool.wait_ge(w_in[i], 16)
                nc.gpsimd.tensor_copy(w_hi[:, i, :], w_full[:, i, :]).then_inc(w_hi_vg_ready, 1)
            for b in range(B):
                nc.gpsimd.memset(state[b][:], 0.0).then_inc(zeroed, 1)
            nc.gpsimd.memset(ones_bf[:], 1.0).then_inc(route_fill, 1)
            pool.wait_ge(route_fill, 1)
            nc.gpsimd.affine_select(out=before[:], in_=ones_bf[:], compare_op=ALU.is_gt, fill=0.0, base=0,
                                    pattern=[[1, P]], channel_multiplier=-1).then_inc(route_consts, 1)

            def numbers(dst, pattern, base=0, per_row=0):
                nc.gpsimd.iota(dst, pattern=pattern, base=base, channel_multiplier=per_row,
                               allow_small_or_imprecise_dtypes=True).then_inc(route_consts, 1)

            numbers(iota_e[:], [[1, E]])
            for dst in (seen, lot_start):
                numbers(dst[:], [[B * T, E // 2], [B * T - 1, 2]])
            numbers(way[:], [[0, E // 2], [-2, 2]], 1)
            for b in range(B):
                numbers(row_no[:, b::2, :], [[P, NR], [0, 1]], T * b, 1)
            numbers(place_no[:], [[P, TILES]], 0, 1)
            numbers(edge_no[:], [[P - 1, 2], [P, TILES]])
            numbers(job_no[:], [[1, 1]], 0, 1)
            numbers(seat_no[:], [[1, SEATS]])

            def divide(n, g):
                pool.wait_ge(num_ready, 4 * n + g + 1)
                after(pool, pe_ot, 2 * n - 1 + g // 2)
                nc.gpsimd.tensor_tensor(og[:, 4 * g:4 * g + 4, :], num[g % 2][:],
                                        rden[g % 2][:].broadcast_to([P, 4, HD]), ALU.mult).then_inc(og_ready, 1)

            def deviation(n):
                pool.wait_ge(mv_ready, n + 1)
                nc.gpsimd.tensor_tensor(veps[:], mv[:, 1:2], eps[:], ALU.add).then_inc(veps_ready, 1)
                pool.wait_ge(veps_ready, n + 1)
                nc.gpsimd.tensor_tensor(rstd[:], veps[:], minus_half[:], ALU.pow).then_inc(rstd_ready, 1)

            def half(r, b):
                n = 2 * r + b
                if b or not isinstance(r, int) or r:
                    deviation(n - 1)
                divide(n, 0)
                if not isinstance(r, int) or r:
                    store_lot(n - 2, b)
                for g in range(1, GROUPS):
                    divide(n, g)

            def store_lot(n, b):
                wait_alone(pool, pool_consts, 2, (placed, n + 1))
                nc.gpsimd.indirect_dma_start(lots, bass.IndirectOffsetOnAxis(ap=place[b][:], axis=0), x1[b][:], None,
                                             bounds_check=LOTS - 1, oob_is_err=True).then_inc(x1_out[b], 16)

            nc.gpsimd.memset(pe_words[:], 0).then_inc(route_consts, 1)
            nc.gpsimd.memset(rows_all[:], 0.0).then_inc(rows_zeroed, 1)
            nc.gpsimd.memset(up_to_e[:], 1.0).then_inc(route_fill, 1)
            nc.gpsimd.memset(lower_t[:], 1.0).then_inc(route_fill, 1)
            pool.wait_ge(route_fill, 3)
            nc.gpsimd.affine_select(out=up_to_e[:], in_=up_to_e[:], compare_op=ALU.is_ge, fill=0.0, base=0,
                                    pattern=[[1, E], [-1, E]], channel_multiplier=0).then_inc(route_consts, 1)
            nc.gpsimd.affine_select(out=lower_t[:], in_=lower_t[:], compare_op=ALU.is_gt, fill=0.0, base=0,
                                    pattern=[[1, TILES], [-1, TILES]], channel_multiplier=0).then_inc(route_consts, 1)

            pool.wait_ge(pool_consts, 2)
            half(0, 0)
            pool.wait_ge(b2_in, 16)
            pool.wait_ge(w_ready, 8)
            nc.gpsimd.affine_select(out=b2_by_tile, in_=b2_rows[:].unsqueeze(1).broadcast_to([P, TILES, D]),
                                    compare_op=ALU.is_ge, fill=0.0, base=0, pattern=[[-E, TILES], [0, D]],
                                    channel_multiplier=1).then_inc(b2_spread, 1)
            pool.wait_ge(b2_spread, 1)
            nc.gpsimd.affine_select(out=b2_by_tile, in_=b2_by_tile, compare_op=ALU.is_ge, fill=0.0, base=E - 1,
                                    pattern=[[E, TILES], [0, D]], channel_multiplier=-1).then_inc(b2_spread, 1)
            half(0, 1)
            pool.wait_ge(lots_zeroed, 16 * (E // 2))
            with pool.Fori(1, NR) as r:
                for b in range(B):
                    half(r, b)

            store_lot(NH - 2, 0)
            deviation(NH - 1)
            store_lot(NH - 1, 1)

            def deviation2(k):
                pool.wait_ge(mv2_ready, k + 1)
                nc.gpsimd.tensor_tensor(veps[:], mv[:, 1:2], eps[:], ALU.add).then_inc(veps2_ready, 1)
                pool.wait_ge(veps2_ready, k + 1)
                nc.gpsimd.tensor_tensor(rstd[:], veps[:], minus_half[:], ALU.pow).then_inc(rstd2_ready, 1)

            def scatter(t, i):
                wait_alone(pool, pool_consts, 2, (idx_to_ready, t + 1), (y2_ready, t + 1))
                nc.gpsimd.indirect_dma_start(out_rows, bass.IndirectOffsetOnAxis(ap=idx_to[i][:], axis=0), y2[i][:], None,
                                             bounds_check=B * T - 1, oob_is_err=True).then_inc(y2_out[i], 16)

            pool.wait_ge(indices_ready, 1)
            for b in range(B):
                pool.wait_ge(x1_out[b], 16 * NR)
            for t in range(TILES + 3):
                if t >= 3:
                    pool.wait_ge(rows_in[t % 3], 16 * (t // 3))
                nc.gpsimd.tensor_copy(idx_g[t % 3][:], idx_from[:, t:t + 1] if t < TILES else idx_from[:, 0:1])\
                    .then_inc(idx_g_ready, 1)
                if t < TILES:
                    pool.wait_ge(idx_g_ready, t + 1)
                    nc.gpsimd.indirect_dma_start(rows_all[:, t, :], None, lots, bass.IndirectOffsetOnAxis(ap=idx_g[t % 3][:], axis=0),
                                                 bounds_check=LOTS - 1, oob_is_err=True).then_inc(rows_in[t % 3], 16)

            with pool.Fori(0, TILES // 2) as i:
                for c in range(2):
                    deviation2(2 * i + c)
                    scatter(2 * i + c, c)

        @block.scalar
        def _(act):
            def weights(i):
                act.wait_ge(w_in[i], 32)
                nc.scalar.activation(w_hi[:, i, :], w_full[:, i, :], ACT.Copy).then_inc(w_hi_ready, 1)

            def exps(r, f):
                act.wait_ge(pe_qk, 8 * r + f + 1)
                after(act, qk_ready, 8 * r + f - 1)
                nc.scalar.activation(expo[f % 2][:], ps_p[f % 2][:], ACT.Exp)
                nc.scalar.activation(relu[f % 2][:], ps_p[f % 2][:], ACT.Relu).then_inc(exp_done, 1)

            def values(m, b, j):
                act.wait_ge(pe_v, 2 * m + j + 1)
                nc.scalar.activation(v1[b][:, 8 * j:8 * j + 8, 0:HD],
                                     ps_p[j % 2][:].rearrange("p (h d) -> p h d", d=HD), ACT.Copy).then_inc(v_ready, 1)

            def gates(m, b, j):
                act.wait_ge(pe_g, 2 * m + j + 1)
                nc.scalar.activation(gate[b][:, 8 * j:8 * j + 8, :],
                                     ps_p[j % 2][:].rearrange("p (h d) -> p h d", d=HD), ACT.Tanh, scale=0.5).then_inc(gate_ready, 1)

            def keys(n, j):
                act.wait_ge(pe_kt, 2 * n + j + 1)
                nc.scalar.activation(ktok[:, 4 * j:4 * j + 4, :], ps_t[:].rearrange("p (a s) -> p a s", s=P),
                                     ACT.Copy).then_inc(ktok_ready, 1)

            def outs(n, j):
                act.wait_ge(pe_ot, 2 * n + j + 1)
                after(act, pe_y, n)
                nc.scalar.activation(ogt[:, 4 * j:4 * j + 4, :], ps_t[:].rearrange("p (a s) -> p a s", s=P),
                                     ACT.Copy).then_inc(ogt_ready, 1)

            def half(r, b, first, ahead):
                n = 2 * r + b
                if b == 1:
                    outs(n - 1, 0)
                    if ahead:
                        exps(r + 1, 0)
                if b == 1 or not first:
                    outs(n - 1, 1)
                if b == 1 and ahead:
                    exps(r + 1, 1)
                if b == 0:
                    values(n + 1, 1, 0)
                    if ahead:
                        keys(n, 0)
                    values(n + 1, 1, 1)
                    if ahead:
                        keys(n, 1)
                    gates(n + 1, 1, 0)
                    gates(n + 1, 1, 1)
                    return
                if ahead:
                    keys(n, 0)
                    keys(n, 1)
                    for f in range(2, PAIRS):
                        exps(r + 1, f)
                outs(n, 0)
                if ahead:
                    for j in range(2):
                        values(n + 1, 0, j)
                    for j in range(2):
                        gates(n + 1, 0, j)

            weights(0)
            weights(1)
            for i in range(GROUPS):
                exps(0, 2 * i)
                exps(0, 2 * i + 1)
                if i + 2 < GROUPS:
                    weights(i + 2)
            act.wait_ge(ones_set, 2)
            for j in range(2):
                values(0, 0, j)
            for j in range(2):
                gates(0, 0, j)
            half(0, 0, True, True)
            half(0, 1, True, True)
            with act.Fori(1, NR - 1) as r:
                for b in range(B):
                    half(r, b, False, True)
            for b in range(B):
                half(NR - 1, b, False, False)
            outs(NH - 1, 1)

            act_registers = [act.alloc_register(f"act_plan{i}") for i in range(2)]

            def experts_of(step):
                return load(act, act_registers, act_words[0:1, bass.ds(step.u, 1), 0:2].rearrange("p o c -> p (o c)"), [E - 1] * 2)

            def fetch(job, e):
                j, i = job.j, job.slot4
                after(act, pe_h, j - 3)
                after(act, hid_ready[job.slot2], job.before - 1)
                nc.scalar.activation(b1_now[i][:], b1_tab[:, bass.ds(e, 1), :].rearrange("p o f -> p (o f)"), ACT.Copy)
                nc.scalar.activation(w1_now[i][:], w1_tab[:, bass.ds(e, 1), :].rearrange("p o f -> p (o f)"),
                                     ACT.Copy).then_inc(w1_now_ready, 1)

            def keep_turned(t):
                act.wait_ge(rows_turned, t + 1)
                nc.scalar.activation(xt_all[:, bass.ds(t, 1), :].rearrange("p o r -> p (o r)"), ps_t[:, 0:P],
                                     ACT.Copy).then_inc(xt_all_ready, 1)

            def keep(step):
                t = step.u
                act.wait_ge(idx_g_ready, t + 4)
                after(act, rows_turned, t - 1)
                nc.scalar.activation(xg[step.slot][:], rows_all[:, bass.ds(t, 1), 0:D].rearrange("p o d -> p (o d)"),
                                     ACT.Copy).then_inc(rows_kept, 1)

            def hidden(job):
                j = job.j
                act.wait_ge(w1_now_ready, j + 1)
                after(act, pe_f, j - 3)
                act.wait_ge(pe_h, j + 1)
                for f in range(FB):
                    cols = slice(f * P, f * P + P)
                    last = nc.scalar.activation(hid[job.slot4][:, cols], ps_p[0][:, cols], ACT.Relu,
                                                bias=b1_now[job.slot4][:, f:f + 1])
                last.then_inc(hid_ready[0], 1)

            def body(step):
                if step.job(2).exists():
                    pair = experts_of(step.plus(1))
                    fetch(step.job(2), pair[0])
                if step.plus(1).of_tile():
                    keep_turned(step.u + 1)
                if step.plus(2).of_tile():
                    keep(step.plus(2))
                if step.job(0).exists():
                    hidden(step.job(0))
                if step.job(3).exists():
                    fetch(step.job(3), pair[1])

            act.wait_ge(weights_turned, 1)
            nc.scalar.activation(expert_weight_t[:], ps_m[:, 0:P], ACT.Copy).then_inc(weights_t_ready, 1)
            act.wait_ge(b1_ready, 1)
            act.wait_ge(w1_in, 16)
            act.wait_ge(plan_ready, 1)
            pair = experts_of(Step(0, 0))
            fetch(Step(0, 0).job(0), pair[0])
            keep(Step(0, 0))
            keep_turned(0)
            fetch(Step(0, 0).job(1), pair[1])
            keep(Step(0, 1))
            all_steps(act, body)

        @block.vector
        def _(dve):
            def split_x(r):
                dve.wait_ge(pe_xt, r + 1)
                turned = ps_m[:, P:(B + 1) * P].rearrange("p (b t) -> p b t", b=B)
                nc.vector.tensor_copy(xt_hi[:], turned).then_inc(xt_half, 1)
                dve.wait_ge(xt_half, r + 1)
                nc.vector.tensor_tensor(xt_lo[:], turned, xt_hi[:].bitcast(F32), ALU.subtract).then_inc(xt_ready, 1)

            def rows(r, f):
                dve.wait_ge(exp_done, 8 * r + f + 1)
                nc.vector.scalar_tensor_tensor(qk[:, f, :, :, :].rearrange("p a b t -> p (a b t)"), expo[f % 2][:], 1.0,
                                               relu[f % 2][:], ALU.min, ALU.add).then_inc(qk_ready, 1)

            def mask(n, g):
                dve.wait_ge(pe_s, 4 * n + g + 1)
                after(dve, pe_o, 4 * n + g - 1)
                for i in range(2):
                    last = nc.vector.tensor_tensor(probs[g % 2][:, i::2, :], ps_s[i][:, 0:2 * P].rearrange("p (h t) -> p h t", t=P),
                                                   causal[:].unsqueeze(1).broadcast_to([P, 2, P]), ALU.mult)
                last.then_inc(probs_ready, 1)

            def numerator(n, b, g):
                i = 4 * n + g
                heads = ps_o[g % 2][:, 0:4 * VW].rearrange("p (h d) -> p h d", d=VW)
                dve.wait_ge(pe_o, i + 1)
                after(dve, og_ready, i - 1)
                nc.vector.tensor_scalar(den[g % 2][:], heads[:, :, HD:VW], 2.0, 2 * DEN_EPS, ALU.mult, ALU.add).then_inc(den_ready, 1)
                dve.wait_ge(den_ready, i + 1)
                nc.vector.reciprocal(rden[g % 2][:], den[g % 2][:]).then_inc(rden_ready, 1)
                dve.wait_ge(gate_ready, 2 * n + g // 2 + 1)
                nc.vector.scalar_tensor_tensor(num[g % 2][:], gate[b][:, 4 * g:4 * g + 4, :], 1.0,
                                               heads[:, :, 0:HD], ALU.add, ALU.mult).then_inc(num_ready, 1)

            def add_state(n, b, i, first):
                a, k = KV_LOTS[i]
                dve.wait_ge(pe_kv, 3 * n + i + 1)
                if first:
                    dve.wait_ge(zeroed, 2)
                else:
                    dve.wait_ge(state_ready, 3 * n + i - 5)
                for h, part in enumerate((slice(0, HD), slice(HD, P))):
                    lot = state[b][part, a:a + k, h, :]
                    new = ps_t[part, 0:2 * VW * k].rearrange("p (a h d) -> p a h d", h=2, d=VW)[:, :, h, :]
                    if first:
                        last = nc.vector.tensor_copy(lot, new)
                    else:
                        last = nc.vector.tensor_tensor(lot, new, lot, ALU.add)
                last.then_inc(state_ready, 1)

            def norm(r, b):
                n = 2 * r + b
                dve.wait_ge(pe_y, n + 1)
                dve.wait_ge(x_res_sem[b], 16 * r + 16)
                nc.vector.tensor_tensor(z[:], ps_m[:, 0:P], x_res[b][:], ALU.add).then_inc(z_ready, 1)
                dve.wait_ge(z_ready, n + 1)
                nc.vector.bn_stats(stats[:], z[:]).then_inc(stats_ready, 1)
                dve.wait_ge(consts, 1)
                dve.wait_ge(stats_ready, n + 1)
                nc.vector.bn_aggr(mv[:], stats[:]).then_inc(mv_ready, 1)
                after(dve, x1_out[b], 16 * r)
                nc.vector.tensor_copy(x1[b][:, D:D + 1], row_no[:, bass.ds(n, 1), :].rearrange("p o d -> p (o d)"))\
                    .then_inc(x1_ready, 1)
                dve.wait_ge(rstd_ready, n + 1)
                nc.vector.tensor_scalar(x1[b][:, 0:D], z[:], mv[:, 0:1], rstd[:, 0:1], ALU.subtract, ALU.mult).then_inc(x1_ready, 1)

            def group_rows(n, b, part):
                v = nc.vector
                done = STAGES * n
                if part == 0:
                    dve.wait_ge(x1_ready, 2 * n + 2)
                    after(dve, grouped, done)
                    v.tensor_tensor(rt_sum[:], x1[b][:, 0:1], x1[b][:, 1:2], ALU.add).then_inc(grouped, 1)
                    dve.wait_ge(grouped, done + 1)
                    v.scalar_tensor_tensor(rt_abs[:], rt_sum[:], -1.0, rt_sum[:], ALU.mult, ALU.max).then_inc(grouped, 1)
                    v.scalar_tensor_tensor(rt_int[:], rt_sum[:], -1.0, rt_sum[:], ALU.mult, ALU.max).then_inc(grouped, 1)
                    v.tensor_scalar(rt_sign[:], rt_sum[:], 0.0, 2.0, ALU.is_lt, ALU.mult).then_inc(grouped, 1)
                elif part == 1:
                    dve.wait_ge(grouped, done + 4)
                    v.scalar_tensor_tensor(rt_whole[:], rt_int[:], rt_abs[:, 0:1], rt_int[:], ALU.is_gt, ALU.subtract)\
                        .then_inc(grouped, 1)
                    dve.wait_ge(grouped, done + 5)
                    v.scalar_tensor_tensor(rt_signed[:], rt_sign[:], -1.0, rt_whole[:], ALU.add, ALU.mult).then_inc(grouped, 1)
                else:
                    dve.wait_ge(grouped, done + 6)
                    v.tensor_scalar(rt_low[:], rt_signed[:], E - 1, None, ALU.bitwise_and).then_inc(grouped, 1)
                    dve.wait_ge(grouped, done + 7)
                    after(dve, placed, n)
                    v.tensor_tensor(onehot[:], rt_low[:].broadcast_to([P, E]), iota_e[:], ALU.is_equal).then_inc(grouped, 1)
                    dve.wait_ge(grouped, done + 8)
                    v.tensor_tensor(signed[:], onehot[:], way[:], ALU.mult).then_inc(grouped, 1)

            def place_rows(n, b):
                v = nc.vector
                dve.wait_ge(ranked, n + 1)
                after(dve, seen_ready, n)
                after(dve, spotted, 3 * n)
                v.tensor_tensor(spot[:], ps_s[0][:, RANKS:RANKS + E], seen[:], ALU.add).then_inc(spotted, 1)
                dve.wait_ge(spotted, 3 * n + 1)
                v.tensor_tensor(spot_own[:], spot[:], onehot[:], ALU.mult).then_inc(spotted, 1)
                v.tensor_tensor(seen[:], ps_s[0][:, RANKS + E:RANKS + 2 * E], seen[:], ALU.add).then_inc(seen_ready, 1)
                dve.wait_ge(spotted, 3 * n + 2)
                v.tensor_reduce(place_f[:], spot_own[:], AX.X, ALU.add).then_inc(spotted, 1)
                dve.wait_ge(spotted, 3 * n + 3)
                v.tensor_copy(place[b][:], place_f[:]).then_inc(placed, 1)

            def half(r, b, first, ahead):
                n = 2 * r + b
                start = first and b == 0
                project = ahead and b == 1
                mask(n, 0)
                mask(n, 1)
                if not start:
                    norm(r - 1 + b, 1 - b)
                numerator(n, b, 0)
                if not start:
                    group_rows(n - 1, 1 - b, 0)
                if project:
                    rows(r + 1, 0)
                mask(n, 2)
                if project:
                    rows(r + 1, 1)
                numerator(n, b, 1)
                if not start:
                    group_rows(n - 1, 1 - b, 1)
                if project:
                    rows(r + 1, 2)
                if ahead:
                    add_state(n, b, 0, first)
                mask(n, 3)
                if project:
                    rows(r + 1, 3)
                if not start:
                    group_rows(n - 1, 1 - b, 2)
                numerator(n, b, 2)
                if project:
                    rows(r + 1, 4)
                if ahead:
                    add_state(n, b, 1, first)
                if not start:
                    place_rows(n - 1, 1 - b)
                if project:
                    rows(r + 1, 5)
                numerator(n, b, 3)
                if ahead:
                    add_state(n, b, 2, first)
                if project:
                    rows(r + 1, 6)
                    rows(r + 1, 7)
                if ahead and b == 0:
                    split_x(r + 1)

            def low_weights(i):
                dve.wait_ge(*((w_hi_ready, i + 1) if i < GROUPS else (w_hi_vg_ready, i - GROUPS + 1)))
                nc.vector.tensor_tensor(w_lo[:, i, :], w_full[:, i, :], w_hi[:, i, :].bitcast(F32), ALU.subtract).then_inc(w_ready, 1)

            dve.wait_ge(consts, 2)
            split_x(0)
            low_weights(0)
            low_weights(1)
            for f in range(PAIRS):
                rows(0, f)
                if f in (1, 3):
                    low_weights(2 + f // 2)
                if f >= 4:
                    low_weights(f)
            half(0, 0, True, True)
            dve.wait_ge(route_consts, 14)
            half(0, 1, True, True)
            for b in range(B):
                half(1, b, False, True)
            with dve.Fori(2, NR - 1) as r:
                for b in range(B):
                    half(r, b, False, True)
            for b in range(B):
                half(NR - 1, b, False, False)
            norm(NR - 1, 1)

            for part in range(3):
                group_rows(NH - 1, 1, part)
            dve.wait_ge(b1_turned, 1)
            nc.vector.tensor_copy(b1_tab[:].rearrange("p e f -> p (e f)"), ps_o[0][:, 0:E * FB]).then_inc(b1_ready, 1)
            place_rows(NH - 1, 1)

            v = nc.vector
            stage = [0]

            def stage_of(*instructions):
                stage[0] += 1
                instructions[-1].then_inc(planned, 1)
                dve.wait_ge(planned, stage[0])

            def along_e(ap, n):
                return ap.unsqueeze(1).broadcast_to([P, n, E])

            def along_t(ap, n):
                return ap.unsqueeze(2).broadcast_to([P, ap.shape[1], n])

            dve.wait_ge(seen_ready, NH)
            stage_of(v.tensor_tensor(span[:], seen[:], lot_start[:], ALU.subtract))
            stage_of(v.tensor_tensor(count[:], span[:], way[:], ALU.mult))
            stage_of(v.tensor_tensor(part_e[:], up_to_e[:], along_e(count[:], E), ALU.mult))
            stage_of(v.tensor_reduce(end[:], part_e[:], AX.X, ALU.add))
            edges = edge_no[:].rearrange("p a t -> p (a t)")
            stage_of(v.tensor_tensor(past_end[:], along_t(place_no[:], E), along_e(end[:], TILES), ALU.is_ge),
                     v.tensor_tensor(past_edge[:].rearrange("p a t e -> p (a t) e"), along_t(edges, E), along_e(end[:], 2 * TILES),
                                     ALU.is_ge),
                     v.tensor_tensor(first[:], end[:], count[:], ALU.subtract))
            stage_of(v.tensor_reduce(group[:], past_end[:], AX.X, ALU.add),
                     v.tensor_reduce(edge[:].rearrange("p a t -> p (a t)"), past_edge[:].rearrange("p a t e -> p (a t) e"),
                                     AX.X, ALU.add),
                     v.tensor_tensor(first_way[:], first[:], way[:], ALU.mult))
            stage_of(v.tensor_tensor(own[:], along_e(iota_e[:], TILES), along_t(group[:], E), ALU.is_equal),
                     v.scalar_tensor_tensor(jobs_of[:], edge[:, 1, :], 2.0, edge[:, 0, :], ALU.add, ALU.subtract),
                     v.tensor_tensor(origin[:], lot_start[:], first_way[:], ALU.subtract))
            stage_of(v.tensor_tensor(own_way[:], own[:], along_e(way[:], TILES), ALU.mult),
                     v.tensor_tensor(own_origin[:], own[:], along_e(origin[:], TILES), ALU.mult),
                     v.tensor_tensor(part_t[:], lower_t[:], jobs_of[:].unsqueeze(1).broadcast_to([P, TILES, TILES]), ALU.mult))
            stage_of(v.tensor_reduce(row_way[:], own_way[:], AX.X, ALU.add),
                     v.tensor_reduce(row_origin[:], own_origin[:], AX.X, ALU.add),
                     v.tensor_reduce(first_job[:], part_t[:], AX.X, ALU.add),
                     v.scalar_tensor_tensor(turn[:, 1:TILES], edge[:, 0, 1:TILES], -2.0, edge[:, 1, 0:TILES - 1],
                                            ALU.add, ALU.subtract),
                     v.tensor_copy(turn[:, 0:1], edge[:, 0, 0:1]))
            stage_of(v.tensor_tensor(along[:], row_way[:], place_no[:], ALU.mult),
                     v.tensor_scalar(past_job[:], first_job[:], job_no[:, 0:1], None, ALU.is_le))
            v.tensor_tensor(idx_from[:], along[:], row_origin[:], ALU.add).then_inc(indices_ready, 1)
            stage_of(v.tensor_tensor(turned_by[:], past_job[:], turn[:], ALU.mult),
                     v.tensor_reduce(job_tile[:], past_job[:], AX.X, ALU.add),
                     v.tensor_tensor(from_seat[:], seat_no[:].unsqueeze(1).broadcast_to([P, TILES, SEATS]),
                                     along_t(group[:], SEATS), ALU.subtract))
            stage_of(v.tensor_reduce(job_turn[:], turned_by[:], AX.X, ALU.add),
                     v.scalar_tensor_tensor(near[:], from_seat[:], -1.0, from_seat[:], ALU.add, ALU.mult))
            stage_of(v.tensor_tensor(job_seat[:], job_turn[:], job_no[:], ALU.add),
                     v.tensor_tensor(job_seat_int[:], job_turn[:], job_no[:], ALU.add),
                     v.tensor_scalar(weight[:, 0:TILES * SEATS], near[:].rearrange("p t e -> p (t e)"), 0.0, 0.5, ALU.is_equal, ALU.mult))
            by_seat = weight[:, 0:TILES * SEATS].rearrange("p (t e) -> p t e", e=SEATS)
            v.tensor_tensor(expert_weight[:], by_seat[:, :, 0:E], by_seat[:, :, E:SEATS], ALU.add).then_inc(weights_set, 1)
            stage_of(v.tensor_scalar(job_plan[:, 0:1], job_tile[:], -1.0, None, ALU.add),
                     v.scalar_tensor_tensor(job_plan[:, 2:3], job_tile[:], float(SEATS), job_seat[:], ALU.mult, ALU.add),
                     v.tensor_scalar(job_low[:], job_seat_int[:], E - 1, None, ALU.bitwise_and))
            v.tensor_copy(job_plan[:, 1:2], job_low[:]).then_inc(jobs_planned, 1)
            dve.wait_ge(plan_turned, 1)
            stage_of(v.tensor_copy(plan[:], ps_s[0][0:1, 0:3 * P].rearrange("p (a j) -> p a j", j=P)[:, :, 0:2 * PLANNED]))
            tile_of, expert_of, weight_of = (plan[:, a, :].rearrange("p (u c) -> p u c", c=2) for a in range(3))
            v.tensor_copy(act_words[:, :, 0:2], expert_of)
            v.tensor_scalar(pe_words[:, 0:PLANNED, 0:2], tile_of, float(P), None, ALU.mult)
            v.tensor_scalar(pe_words[:, 1:PLANNED + 1, 2:4], expert_of, float(FB * D), None, ALU.mult)
            v.tensor_scalar(dve_words[:, :, 0:2], tile_of, float(P), None, ALU.mult)
            v.tensor_scalar(dve_words[:, :, 2:4], weight_of, -float(SEATS), None, ALU.add).then_inc(plan_ready, 1)

            def keep_biases(a):
                dve.wait_ge(bias_made, a + 1)
                v.tensor_copy(bias_all[:, 4 * a:4 * a + 4, :].rearrange("p t d -> p (t d)"), bias_banks[a % 2][:])\
                    .then_inc(bias_ready, 1)

            keep_biases(0)

            def base(step):
                t = step.u
                if isinstance(t, int) and t < 4:
                    dve.wait_ge(bias_ready, 1)
                dve.wait_ge(idx_g_ready, t + 4)
                v.tensor_tensor(acc[:, bass.ds(t, 1), :], rows_all[:, bass.ds(t, 1), 0:D], bias_all[:, bass.ds(t, 1), :],
                                ALU.add).then_inc(based, 1)

            dve_registers = [dve.alloc_register(f"dve_plan{i}") for i in range(4)]

            def weights_of(step):
                words = load(dve, dve_registers, dve_words[0:1, bass.ds(step.u, 1), :].rearrange("p o c -> p (o c)"),
                             [TILES * P - P] * 2 + [TILES * SEATS] * 2)
                return [words[0::2], words[1::2]]

            def hidden(job):
                j, i = job.j, job.slot4
                dve.wait_ge(w1_now_ready, j + 1)
                after(dve, pe_f, j - 3)
                dve.wait_ge(pe_h, j + 1)
                for f in range(FB):
                    cols = slice(f * P, f * P + P)
                    last = v.tensor_scalar(hid[i][:, cols], ps_p[1][:, cols], b1_now[i][:, f:f + 1], 0.0, ALU.add, ALU.max)
                last.then_inc(hid_ready[1], 1)

            def add(job, step, where):
                j, i = job.j, job.slot2
                start, w = where
                rows_of = acc[:].rearrange("p t d -> p (t d)")[:, bass.ds(start, P)]
                wait_alone(dve, plan_ready, 1, (based, step.u if step.of_tile() else TILES), (added, j), (pe_f, j + 1))
                v.scalar_tensor_tensor(rows_of, ps_o[i][:, 0:P], weight[:, bass.ds(w, 1)], rows_of, ALU.mult, ALU.add).then_inc(added, 1)

            def moments(step):
                t, i = step.u, step.slot
                rows_of = acc[:, bass.ds(t, 1), :].rearrange("p o d -> p (o d)")
                number = rows_all[:, bass.ds(t, 1), D:D + 1].rearrange("p o d -> p (o d)")
                after(dve, y2_out[i], 16 * (step.i + step.c // 2))
                v.tensor_copy(idx_to[i][:], number).then_inc(idx_to_ready, 1)
                dve.wait_ge(added, 2 * t + 2 * LAG + 1)
                v.bn_stats(stats[:], rows_of).then_inc(stats2_ready, 1)
                if not isinstance(t, int) or t:
                    wait_alone(dve, plan_ready, 1, (y2_ready, t))
                wait_alone(dve, plan_ready, 1, (stats2_ready, t + 1))
                v.bn_aggr(mv[:], stats[:]).then_inc(mv2_ready, 1)

            def finish(step):
                t, i = step.u, step.slot
                rows_of = acc[:, bass.ds(t, 1), :].rearrange("p o d -> p (o d)")
                dve.wait_ge(rstd2_ready, t + 1)
                v.tensor_scalar(y2[i][:], rows_of, mv[:, 0:1], rstd[:, 0:1], ALU.subtract, ALU.mult).then_inc(y2_ready, 1)

            def body(step):
                ended = step.plus(-LAG - 1)
                if step.job(-2).exists():
                    pair = weights_of(step.plus(-1))
                    add(step.job(-2), step, pair[0])
                if step.job(1).exists():
                    hidden(step.job(1))
                if ended.plus(-1).of_tile():
                    finish(ended.plus(-1))
                if ended.of_tile():
                    moments(ended)
                if isinstance(step.u, int) and step.u < 3:
                    keep_biases(step.u + 1)
                if step.of_tile():
                    base(step)
                if step.job(-1).exists():
                    add(step.job(-1), step, pair[1])

            all_steps(dve, body)

        @block.tensor
        def _(pe):
            def turn_x(r):
                pe.wait_ge(x_in_sem, 16 * r + 16)
                after(pe, z_ready, 2 * r - 2)
                for b in range(B):
                    last = nc.tensor.transpose(ps_m[:, (b + 1) * P:(b + 2) * P], x_in[:, b, :], ident[:])
                last.then_inc(pe_xt, 1)

            def three(dst, pairs):
                for i, (lhs, rhs) in enumerate(pairs):
                    last = nc.tensor.matmul(dst, lhs, rhs, start=(i == 0), stop=(i == 2))
                return last

            def project_qk(r, f):
                if f == 0:
                    pe.wait_ge(xt_ready, r + 1)
                if f < 2:
                    after(pe, gate_ready, 4 * r - 1 + f)
                else:
                    pe.wait_ge(exp_done, 8 * r + f - 1)
                rows = [t[:].rearrange("p b t -> p (b t)") for t in (xt_hi, xt_lo)]
                for i in range(2):
                    cols = slice(256 * i + P * (f % 2), 256 * i + P * (f % 2) + P)
                    hi, lo = w_hi[:, f // 2, cols], w_lo[:, f // 2, cols]
                    last = three(ps_p[f % 2][:, 256 * i:256 * i + 256], [(hi, rows[0]), (hi, rows[1]), (lo, rows[0])])
                last.then_inc(pe_qk, 1)

            def project_vg(r, b, i):
                m, j = 2 * r + b, i % 2
                if i >= 2:
                    pe.wait_ge(v_ready, 2 * m + 1 + j)
                elif b == 0:
                    pe.wait_ge(exp_done, 8 * r + 7 + j)
                else:
                    pe.wait_ge(gate_ready, 4 * r + 1 + j)
                hi, lo = w_hi[:, 4 + i, :], w_lo[:, 4 + i, :]
                three(ps_p[j][:], [(xt_hi[:, b, :], hi), (xt_hi[:, b, :], lo), (xt_lo[:, b, :], hi)])\
                    .then_inc(pe_v if i < 2 else pe_g, 1)

            def scores(r, b, g):
                n = 2 * r + b
                pe.wait_ge(qk_ready, 8 * r + 2 * g + 2)
                if g == 0:
                    after(pe, placed, n - 1)
                after(pe, probs_ready, 4 * n + g)
                for a in range(2):
                    for h, part in enumerate((slice(0, HD), slice(HD, P))):
                        last = nc.tensor.matmul(ps_s[h][:, a * P:a * P + P], qk[part, 2 * g + a, 1, b, :],
                                                qk[part, 2 * g + a, 0, b, :], start=True, stop=True)
                last.then_inc(pe_s, 1)

            def turn_k(n, b, j):
                after(pe, *((ogt_ready, 2 * n) if j == 0 else (ktok_ready, 2 * n + 1)))
                for i in range(4):
                    last = nc.tensor.transpose(ps_t[:, i * P:i * P + P], qk[:, 4 * j + i, 1, b, :], ident[:])
                last.then_inc(pe_kt, 1)

            def attend(n, b, g, first):
                after(pe, num_ready, 4 * n + g - 1)
                pe.wait_ge(v_ready, 2 * n + g // 2 + 1)
                if not first:
                    pe.wait_ge(state_ready, 3 * n - 3)
                pe.wait_ge(probs_ready, 4 * n + g + 1)
                for a in range(2):
                    if not first:
                        nc.tensor.matmul(ps_o[g % 2][:, 2 * VW * a:2 * VW * (a + 1)], qk[:, 2 * g + a, 0, b, :],
                                         state[b][:, 2 * g + a, :, :].rearrange("p h d -> p (h d)"), start=True, stop=False,
                                         skip_group_check=True)
                    for i in range(2 * a, 2 * a + 2):
                        last = nc.tensor.matmul(ps_o[g % 2][:, i * VW:i * VW + VW], probs[g % 2][:, i, :], v1[b][:, 4 * g + i, :],
                                                start=first, stop=True, skip_group_check=True)
                last.then_inc(pe_o, 1)

            def sum_kv(n, b, i):
                a, k = KV_LOTS[i]
                if i == 0:
                    pe.wait_ge(ktok_ready, 2 * n + 2)
                    pe.wait_ge(v_ready, 2 * n + 2)
                else:
                    pe.wait_ge(state_ready, 3 * n + i)
                for j in range(k):
                    last = nc.tensor.matmul(ps_t[:, 2 * VW * j:2 * VW * (j + 1)], ktok[:, a + j, :],
                                            v1[b][:, 2 * (a + j):2 * (a + j) + 2, :].rearrange("p h d -> p (h d)"),
                                            start=True, stop=True)
                last.then_inc(pe_kv, 1)

            def turn_o(n, j, summed=True):
                pe.wait_ge(og_ready, 4 * n + 2 * j + 2)
                if j == 0 and summed:
                    pe.wait_ge(state_ready, 3 * n + 3)
                else:
                    pe.wait_ge(ogt_ready, 2 * n + j)
                for i in range(4):
                    a = 4 * j + i
                    last = nc.tensor.transpose(ps_t[:, i * P:i * P + P],
                                               og[:, 2 * a:2 * a + 2, :].rearrange("p h d -> p (h d)"), ident[:])
                last.then_inc(pe_ot, 1)

            def add_pairs(j):
                for a in range(PAIRS // 2 * j, PAIRS // 2 * (j + 1)):
                    last = nc.tensor.matmul(ps_m[:, 0:P], ogt[:, a, :], wo[:, a, :], start=(a == 0), stop=(a == PAIRS - 1))
                return last

            def project_out(r, b, ahead=True):
                n = 2 * r + b
                pe.wait_ge(ogt_ready, 2 * n + 2)
                if b == 0 and ahead:
                    pe.wait_ge(xt_ready, r + 2)
                else:
                    pe.wait_ge(z_ready, n)
                add_pairs(0)
                add_pairs(1).then_inc(pe_y, 1)

            def rank(n):
                pe.wait_ge(grouped, STAGES * n + STAGES)
                pe.wait_ge(probs_ready, min(4 * n + 8, 4 * NH) if isinstance(n, int) else 4 * n + 8)
                nc.tensor.matmul(ps_s[0][:, RANKS:RANKS + E], before[:], signed[:], start=True, stop=True)
                nc.tensor.matmul(ps_s[0][:, RANKS + E:RANKS + 2 * E], ones_bf[:], signed[:], start=True, stop=True).then_inc(ranked, 1)

            def half(r, b, first, ahead):
                n = 2 * r + b
                start = first and b == 0
                project = ahead and b == 1
                if b == 1:
                    scores(r, b, 0)
                    turn_o(n - 1, 0, ahead)
                if project:
                    project_qk(r + 1, 0)
                if not start:
                    turn_o(n - 1, 1)
                if project:
                    project_qk(r + 1, 1)
                if b == 0:
                    project_vg(r, 1, 0)
                scores(r, b, 1)
                if ahead:
                    turn_k(n, b, 0)
                if not start:
                    project_out(r - 1 + b, 1 - b, ahead)
                if b == 0:
                    project_vg(r, 1, 1)
                if ahead:
                    turn_k(n, b, 1)
                attend(n, b, 0, first)
                if project:
                    project_qk(r + 1, 2)
                scores(r, b, 2)
                attend(n, b, 1, first)
                if ahead:
                    sum_kv(n, b, 0)
                project_qk(r + 1, 3) if project else b or project_vg(r, 1, 2)
                scores(r, b, 3)
                attend(n, b, 2, first)
                if project:
                    project_qk(r + 1, 4)
                if ahead:
                    sum_kv(n, b, 1)
                project_qk(r + 1, 5) if project else b or project_vg(r, 1, 3)
                if not start:
                    rank(n - 1)
                if b == 1 and not ahead:
                    turn_o(n, 0, False)
                attend(n, b, 3, first)
                if ahead:
                    sum_kv(n, b, 2)
                if project:
                    project_qk(r + 1, 6)
                if ahead and b == 0:
                    turn_x(r + 1)
                if project:
                    project_qk(r + 1, 7)
                if project:
                    turn_o(n, 0)
                if project:
                    for i in range(4):
                        project_vg(r + 1, 0, i)
                        if i == 1:
                            scores(r + 1, 0, 0)

            pe.wait_ge(consts, 1)
            turn_x(0)
            for f in range(PAIRS):
                pe.wait_ge(w_ready, f // 2 + 1)
                project_qk(0, f)
            for i in range(4):
                pe.wait_ge(w_ready, 5 + i)
                project_vg(0, 0, i)
            pe.wait_ge(wo_in, 16)
            scores(0, 0, 0)
            for b in range(B):
                half(0, b, True, True)
            with pe.Fori(1, NR - 1) as r:
                for b in range(B):
                    half(r, b, False, True)
            for b in range(B):
                half(NR - 1, b, False, False)
            pe.wait_ge(ogt_ready, 2 * NH - 1)
            pe.wait_ge(z_ready, NH - 1)
            add_pairs(0)
            turn_o(NH - 1, 1)
            pe.wait_ge(ogt_ready, 2 * NH)
            add_pairs(1).then_inc(pe_y, 1)

            pe.wait_ge(b1_in, 16)
            nc.tensor.transpose(ps_o[0][:, 0:E * FB], b1_rows[:], ident[0:E * FB, 0:E * FB]).then_inc(b1_turned, 1)
            rank(NH - 1)

            def sum_biases(a):
                pe.wait_ge(weights_t_ready, 1)
                after(pe, bias_ready, a - 1)
                nc.tensor.matmul(bias_banks[a % 2][:], expert_weight_t[:],
                                 b2_by_tile[:, 4 * a:4 * a + 4, :].rearrange("p t d -> p (t d)"),
                                 start=True, stop=True).then_inc(bias_made, 1)

            def turn_rows(step):
                t = step.u
                pe.wait_ge(rows_kept, t + 1)
                after(pe, xt_all_ready, t)
                nc.tensor.transpose(ps_t[:, 0:P], xg[step.slot][:], ident[:]).then_inc(rows_turned, 1)

            def into_hidden(job, step, start):
                j, i = job.j, job.slot2
                if step.of_tile():
                    pe.wait_ge(xt_all_ready, step.u + 1)
                pe.wait_ge(w1_now_ready, j + 1)
                after(pe, hid_ready[i], job.before)
                rows = xt_all[:].rearrange("p t r -> p (t r)")[:, bass.ds(start, P)]
                for f in range(FB):
                    last = nc.tensor.matmul(ps_p[i][:, f * P:f * P + P], w1_now[job.slot4][:, f * P:f * P + P], rows,
                                            start=True, stop=True)
                last.then_inc(pe_h, 1)

            def out_of_hidden(job, table):
                j, i = job.j, job.slot2
                after(pe, added, j - 1)
                pe.wait_ge(hid_ready[i], job.before + 1)
                for f in range(FB):
                    last = nc.tensor.matmul(ps_o[i][:, 0:P], hid[job.slot4][:, f * P:f * P + P],
                                            w2_tab[:].rearrange("p e f d -> p (e f d)")[:, bass.ds(table + f * D, D)],
                                            start=(f == 0), stop=(f == FB - 1))
                last.then_inc(pe_f, 1)

            pe_registers = [pe.alloc_register(f"pe_plan{i}") for i in range(4)]

            def body(step):
                if not isinstance(step.u, int) or step.u <= PLANNED:
                    words = load(pe, pe_registers, pe_words[0:1, bass.ds(step.u, 1), :].rearrange("p o c -> p (o c)"),
                                 [TILES * P - P] * 2 + [(E - 1) * FB * D] * 2)
                first = isinstance(step.u, int) and step.u == 0
                if step.plus(1).of_tile() and not first:
                    turn_rows(step.plus(1))
                for c in range(2):
                    if step.job(c).exists():
                        into_hidden(step.job(c), step, words[c])
                    if step.job(c - 2).exists():
                        out_of_hidden(step.job(c - 2), words[2 + c])
                if first:
                    turn_rows(step.plus(1))
                if isinstance(step.u, int) and step.u < 2:
                    sum_biases(step.u + 2)

            pe.wait_ge(b1_ready, 1)
            pe.wait_ge(weights_set, 1)
            nc.tensor.transpose(ps_m[:, 0:P], expert_weight[:].rearrange("p t e -> p (t e)"), ident[:]).then_inc(weights_turned, 1)
            pe.wait_ge(jobs_planned, 1)
            pe.wait_ge(placed, NH)
            for a in range(3):
                last = nc.tensor.transpose(ps_s[0][0:1, a * P:a * P + P], job_plan[:, a:a + 1], ident[:])
            last.then_inc(plan_turned, 1)
            pe.wait_ge(b2_spread, 2)
            sum_biases(0)
            sum_biases(1)
            turn_rows(Step(0, 0))
            pe.wait_ge(plan_ready, 1)
            pe.wait_ge(w2_in, 16)
            all_steps(pe, body)


_INS = ["L0_attn_x", "L0_attn_w_qkv", "L0_attn_w_gate", "L0_attn_w_out",
        "L0_ffn_W1", "L0_ffn_b1", "L0_ffn_W2", "L0_ffn_b2"]
_OUTS = [((2, 1024, 128), "float32")]


def kernel(**inputs):
    import numpy as _np
    import concourse.bacc as _bacc
    from concourse import mybir as _mybir
    from concourse.bass_utils import run_bass_kernel_spmd as _run

    nc = _bacc.Bacc("TRN2", target_bir_lowering=False, num_devices=1)
    arrays, args = {}, []
    for name in _INS:
        a = _np.ascontiguousarray(inputs[name])
        arrays[f"in_{name}_dram"] = a
        args.append(nc.dram_tensor(f"in_{name}_dram", a.shape, _mybir.dt.from_np(a.dtype), kind="ExternalInput").ap())
    for i, (shape, dtype) in enumerate(_OUTS):
        dt = _mybir.dt.from_np(_np.dtype(dtype))
        args.append(nc.dram_tensor(f"out_{i}_dram", shape, dt, kind="ExternalOutput").ap())
    build(nc, *args)
    r = _run(nc, [arrays], core_ids=[0])
    got = tuple(r.results[0][f"out_{i}_dram"] for i in range(len(_OUTS)))
    return got[0]
```
